# Optimizing a Trainium2 kernel written in Bass

```python
import numpy as np
import jax
import jax.numpy as jnp

def _softmax(x, axis=-1):
    return jax.nn.softmax(x, axis=axis)

def _gelu(x):
    return jax.nn.gelu(x, approximate=True)

def _silu(x):
    return jax.nn.silu(x)

def _sigmoid(x):
    return jax.nn.sigmoid(x)

def _layernorm(x, axis=-1, eps=1e-05):
    m = jnp.mean(x, axis=axis, keepdims=True)
    v = jnp.var(x, axis=axis, keepdims=True)
    return (x - m) / jnp.sqrt(v + eps)

def _scatter_add(tgt, idx, src, axis=0):
    return tgt.at[idx].add(src)

def _segment_sum(src, seg, n):
    return jax.ops.segment_sum(src, seg, n)
kernel_name = 'mk_gnn_ffn_d1_gnn_r8_297c6f'

def setup_inputs(seed: int=0):
    np.random.seed(seed)
    _w = jnp.asarray

    def _rec_inputs():
        import jax
        import jax.numpy as jnp
        _gk = jax.random.key(seed)
        x = -0.0002117 + 1 * jax.random.normal(jax.random.fold_in(_gk, 1), (12500, 256), jnp.float32)
        src = jax.random.randint(jax.random.fold_in(_gk, 2), (200000,), 0, 12500, jnp.int32)
        dst = jnp.minimum((12500 * jax.random.uniform(jax.random.fold_in(_gk, 3), (200000,)) ** 2.0).astype(jnp.int32), 99999)
        _o = jnp.argsort(dst, stable=True)
        src = src[_o]
        dst = dst[_o]
        edge_weight = jax.random.uniform(jax.random.fold_in(_gk, 12), (200000,), jnp.float32, 0.0, 1)
        return (x, src, dst, edge_weight)
    x, src, dst, edge_weight = _rec_inputs()

    def _L0_gnn_setup():
        import jax, jax.numpy as jnp
        import numpy as np
        N_NODES = 12500
        N_EDGES = 400000
        D_IN = 256
        D_OUT = 256
        key = jax.random.key(seed)
        k1, k2, k3, k4, k5 = jax.random.split(key, 5)
        x = jax.random.normal(k1, (N_NODES, D_IN), dtype=jnp.float32)
        edge_row = jax.random.randint(k2, (N_EDGES,), 0, N_NODES, dtype=jnp.int32)
        edge_col = jax.random.randint(k3, (N_EDGES,), 0, N_NODES, dtype=jnp.int32)
        edge_val = jax.random.uniform(k4, (N_EDGES,), dtype=jnp.float32)
        limit = 1.414 * np.sqrt(6.0 / (D_IN + D_OUT))
        weight = jax.random.uniform(k5, (D_IN, D_OUT), dtype=jnp.float32, minval=-limit, maxval=limit)
        b = jnp.zeros((D_OUT,), dtype=jnp.float32)
        return {'x': x, 'edge_row': edge_row, 'edge_col': edge_col, 'edge_val': edge_val, 'weight': weight, 'b': b}
    _L0_gnn_all = _L0_gnn_setup()
    _L0_gnn_in = {k: v for k, v in _L0_gnn_all.items() if k in ('weight', 'b')}
    del _L0_gnn_all

    def _L0_ffn_setup():
        import jax, jax.numpy as jnp
        import numpy as np
        E = 8
        K = 2
        D = 256
        H = 512
        DOUT = 256
        EPS = 1e-05
        key = jax.random.key(seed)
        ks = jax.random.split(key, 9)
        s = 0.02
        return {'x': jax.random.normal(ks[0], (4, 1024, D), jnp.float32), 'gamma': 1.0 + 0.05 * jax.random.normal(ks[1], (D,), jnp.float32), 'beta': 0.05 * jax.random.normal(ks[2], (D,), jnp.float32), 'Wr': 0.01 * jax.random.normal(ks[3], (D, E), jnp.float32), 'br': jnp.zeros((E,), jnp.float32), 'W1': s * jax.random.normal(ks[4], (E, D, H), jnp.float32), 'b1': s * jax.random.normal(ks[5], (E, H), jnp.float32), 'W2': s * jax.random.normal(ks[6], (E, H, DOUT), jnp.float32), 'b2': s * jax.random.normal(ks[7], (E, DOUT), jnp.float32)}
    _L0_ffn_all = _L0_ffn_setup()
    _L0_ffn_in = {k: v for k, v in _L0_ffn_all.items() if k in ('gamma', 'beta', 'Wr', 'br', 'W1', 'b1', 'W2', 'b2')}
    del _L0_ffn_all
    return {'x': x, 'src': src, 'dst': dst, 'edge_weight': edge_weight, 'L0_gnn_weight': _L0_gnn_in['weight'], 'L0_gnn_b': _L0_gnn_in['b'], 'L0_ffn_gamma': _L0_ffn_in['gamma'], 'L0_ffn_beta': _L0_ffn_in['beta'], 'L0_ffn_Wr': _L0_ffn_in['Wr'], 'L0_ffn_br': _L0_ffn_in['br'], 'L0_ffn_W1': _L0_ffn_in['W1'], 'L0_ffn_b1': _L0_ffn_in['b1'], 'L0_ffn_W2': _L0_ffn_in['W2'], 'L0_ffn_b2': _L0_ffn_in['b2']}

def reference(x, src, dst, edge_weight, L0_gnn_weight, L0_gnn_b, L0_ffn_gamma, L0_ffn_beta, L0_ffn_Wr, L0_ffn_br, L0_ffn_W1, L0_ffn_b1, L0_ffn_W2, L0_ffn_b2):
    import jax
    import jax.numpy as jnp

    def _L0_gnn_ref(x, edge_row, edge_col, edge_val, weight, b):
        import jax, jax.numpy as jnp
        import numpy as np
        N_NODES = 12500
        N_EDGES = 400000
        D_IN = 256
        D_OUT = 256
        h = jnp.matmul(x, weight)
        msgs = edge_val[:, None] * h[edge_col]
        out = jax.ops.segment_sum(msgs, edge_row, num_segments=N_NODES)
        return out + b

    def _L0_ffn_ref(x, gamma, beta, Wr, br, W1, b1, W2, b2):
        import jax, jax.numpy as jnp
        import numpy as np
        E = 8
        K = 2
        D = 256
        H = 512
        DOUT = 256
        EPS = 1e-05
        mu = jnp.mean(x, axis=-1, keepdims=True)
        var = jnp.mean(jnp.square(x - mu), axis=-1, keepdims=True)
        xn = (x - mu) * jax.lax.rsqrt(var + EPS) * gamma + beta
        logits = jnp.einsum('bsd,de->bse', xn, Wr) + br
        top_vals, top_idx = jax.lax.top_k(logits, K)
        w = jax.nn.softmax(top_vals, axis=-1)
        w_full = jnp.einsum('bsk,bske->bse', w, jax.nn.one_hot(top_idx, E, dtype=w.dtype))
        y = jnp.zeros(x.shape[:-1] + (DOUT,), x.dtype)
        for e in range(E):
            h = jax.nn.gelu(jnp.einsum('bsd,dh->bsh', xn, W1[e]) + b1[e], approximate=False)
            y_e = jnp.einsum('bsh,hd->bsd', h, W2[e]) + b2[e]
            y = y + y_e * w_full[..., e, None]
        return y
    x = x + _L0_gnn_ref(_layernorm(x, axis=-1), src, dst, edge_weight, L0_gnn_weight, L0_gnn_b)
    x = x + _L0_ffn_ref(_layernorm(x, axis=-1)[None], L0_ffn_gamma, L0_ffn_beta, L0_ffn_Wr, L0_ffn_br, L0_ffn_W1, L0_ffn_b1, L0_ffn_W2, L0_ffn_b2)[0]
    return x

_drawn_inputs = setup_inputs


def setup_inputs(seed=0):
    import zlib

    import numpy as np

    out = dict(_drawn_inputs(seed))
    spreads = {'L0_gnn_b': (0.0, 0.269), 'L0_ffn_br': (0.0, 0.482)}
    factors = {'L0_ffn_gamma': 8.0,
     'L0_ffn_beta': 8.0,
     'L0_ffn_Wr': 4.912,
     'L0_ffn_W1': 3.61,
     'L0_ffn_b1': 27.379,
     'L0_ffn_W2': 3.503,
     'L0_ffn_b2': 31.511}
    for name, (base, spread) in spreads.items():
        noise = np.random.default_rng([zlib.crc32(name.encode()), seed]).standard_normal(out[name].shape)
        drawn = base * np.exp(spread * noise) if base else spread * noise
        out[name] = jnp.asarray(drawn.astype(out[name].dtype))
    for name, factor in factors.items():
        out[name] = (out[name] * factor).astype(out[name].dtype)
    return out
```

```python
from contextlib import ExitStack

import concourse.bass as bass
from concourse import mybir

F32 = mybir.dt.float32
I32 = mybir.dt.int32
U32 = mybir.dt.uint32
BF16 = mybir.dt.bfloat16
ALU = mybir.AluOpType
ACT = mybir.ActivationFunctionType
AX_X = mybir.AxisListType.X

P = 128
NODES, D = 12500, 256
EDGES = 200000
EXPERTS, HID = 8, 512
EPS = 1e-5
NT = -(-NODES // P)
TAIL = NODES - (NT - 1) * P
KD, KH = D // P, HID // P
PER = 16
COLS = NT * PER
assert COLS * P >= EDGES
LAST = EDGES - (P - 1) * COLS
assert 0 < LAST <= COLS
BINS = NT + 1
GRP = 4
GRPS = PER // GRP
CHAINS = 2 * GRP
STEPS = -(-((EDGES + NT * (P - 1)) // P) // (2 * PER)) * 2
SLOTT = STEPS * PER
NSLOT = SLOTT * P
FAR = 1 << 20
BEYOND = float(1 << 25)
SEG = (2 * NODES + EXPERTS * (P - 1)) // P
ET = SEG + SEG % 2
FILLS = 16
ZROWS = 6
assert ET % ZROWS == 0


def done(steps, name, i):
    return i * len(steps) + steps.index(name) + 1


def rounds(eng, n, body):
    body(0)
    with eng.Fori(1, n - 1) as i:
        body(i)
    body(n - 1)


def is_first(i):
    return isinstance(i, int) and i == 0


def is_last(i, n):
    return isinstance(i, int) and i == n - 1


LN_DVE = ("stats", "aggr", "rstd", "norm")
LN_ACT = ("std", "nT", "h")
LN_PE = ("nT", "h")
POS = ("int", "row", "col", "addr", "rec")
RT_DVE = ("xa", "x1", "stats1", "aggr1", "rstd1", "y", "stats2", "aggr2", "rstd2", "z", "zg", "xn",
          "logits", "top", "index", "indexf", "hot1", "hot2", "vals")
RT_ACT = ("std1", "std2", "keep", "xT")
RT_PE = ("xT", "logits")
EX_PE = ("xT", "up", "hT", "down")
EX_ACT = ("xT", "gelu")
EX_DVE = ("b1", "hT", "b2")


def gnn_moe(nc, x, src, dst, edge_weight, gw, gb, gamma, beta, wr, br, w1, b1, w2, b2, out):
    h_rows = nc.dram_tensor("h_rows", (NT * P, D), F32).ap()
    edges_sorted = nc.dram_tensor("edges_sorted", (NSLOT, 4), I32).ap()
    x1_rows = nc.dram_tensor("x1_rows", (NT * P, D), F32).ap()
    expert_in = nc.dram_tensor("expert_in", (ET * P, D), F32).ap()
    expert_out = nc.dram_tensor("expert_out", (ET * P, D), F32).ap()

    with ExitStack() as ctx:
        def sb(name, shape, dt=F32):
            return ctx.enter_context(nc.sbuf_tensor(name, shape, dt))

        def sem(name):
            return ctx.enter_context(nc.semaphore(name))

        def sem2(name):
            return [sem(f"{name}{i}") for i in range(2)]

        acc = sb("acc", [P, NT, D])
        flat = acc[:, :, :].rearrange("p t d -> p (t d)")
        o1, o2 = EXPERTS * KD * HID, EXPERTS * KD * HID + EXPERTS * KH * D
        w1_sb = flat[:, 0:o1].rearrange("p (e k n) -> p e k n", e=EXPERTS, k=KD)
        w2_sb = flat[:, o1:o2].rearrange("p (e k n) -> p e k n", e=EXPERTS, k=KH)
        b1_sb = flat[:, o2:o2 + EXPERTS * HID].rearrange("p (e n) -> p e n", e=EXPERTS)
        o3 = o2 + EXPERTS * HID
        b2_sb = flat[:, o3:o3 + EXPERTS * D].rearrange("p (e n) -> p e n", e=EXPERTS)
        assert o3 + EXPERTS * D <= NT * D

        recs = sb("recs", [P, COLS, 4], I32)
        recs_f = recs[:, :, :].bitcast(F32)
        binf = recs_f[:, :, 3]
        src_sb, dst_sb = (flat[:, k * COLS:(k + 1) * COLS].bitcast(I32) for k in range(2))
        ew_sb = flat[:, 2 * COLS:3 * COLS]
        ramp_i = flat[:, 3 * COLS:3 * COLS + SLOTT].bitcast(I32)
        late = recs_f.rearrange("p t w -> p (t w)")
        hot1, hot2, texp, slot = (late[:, k * NT * EXPERTS:(k + 1) * NT * EXPERTS]
                                  .rearrange("p (t e) -> p t e", e=EXPERTS) for k in range(4))
        ex_u, ex_h, ex_hT = (late[:, k * 2 * HID:(k + 1) * 2 * HID].rearrange("p (s n) -> p s n", s=2)
                             for k in range(3))
        ex_y, ya1, ya2 = (late[:, 6 * HID + k * 2 * D:6 * HID + (k + 1) * 2 * D]
                          .rearrange("p (s n) -> p s n", s=2) for k in range(3))
        fill = sb("fill", [P, SLOTT // FILLS, 4], I32)
        fill_f = fill[:, :, :].bitcast(F32)
        ramp = sb("ramp", [P, SLOTT])
        past = sb("past", [P, SLOTT], BF16)
        zeros = sb("zeros", [P, ZROWS * D])
        tri = sb("tri", [P, P], BF16)
        rest = sb("rest", [P, P], BF16)
        ones = sb("ones", [P, P], BF16)
        onesf = sb("onesf", [P, P])
        ident = sb("ident", [P, P])
        valid = sb("valid", [P, 1])
        eps = sb("eps", [P, 1])
        gw_sb = sb("gw_sb", [P, KD, D])
        gb_sb = sb("gb_sb", [P, D])
        gamma_sb = sb("gamma_sb", [P, D])
        beta_sb = sb("beta_sb", [P, D])
        wr_sb = sb("wr_sb", [P, KD, EXPERTS])
        br_sb = sb("br_sb", [P, EXPERTS])
        hot = sb("hot", [P, GRPS, GRP, BINS], BF16)
        prod = sb("prod", [P, 2, GRP, BINS])
        rows = sb("rows", [P, PER, D])
        rows_flat = rows[:, :, :].rearrange("p k d -> p (k d)")
        totals, base = (rows_flat[:, k * CHAINS * BINS:(k + 1) * CHAINS * BINS]
                        .rearrange("p (c b) -> p c b", c=CHAINS) for k in range(2))
        binsum = sb("binsum", [P, BINS])
        bintile_i = sb("bintile_i", [P, BINS], I32)
        bintile = sb("bintile", [P, BINS])
        binend = sb("binend", [P, BINS])
        endcol = sb("endcol", [P, 1])
        tile_bin = sb("tile_bin", [1, SLOTT], I32)
        pos = sb("pos", [P, 2, PER])
        pos_i = sb("pos_i", [P, 2, PER], I32)
        pos_row = sb("pos_row", [P, 2, PER], I32)
        pos_col = sb("pos_col", [P, 2, PER], I32)
        addr = sb("addr", [P, 2, PER], I32)
        rec_out = sb("rec_out", [P, 2, PER, 4], I32)
        xin = sb("xin", [P, 2, D])
        stats = sb("stats", [P, 2, 6])
        mv = sb("mv", [P, 2, 2])
        std = sb("std", [P, 2, 1])
        rstd = sb("rstd", [P, 2, 1])
        normed = sb("normed", [P, 2, D])
        normedT = sb("normedT", [P, 2, D])
        h_out = sb("h_out", [P, 2, D])
        rec_in = sb("rec_in", [P, 2, PER, 4], I32)
        rec_in_f = rec_in[:, :, :, :].bitcast(F32)
        pick = sb("pick", [P, 4, P])
        ya = sb("ya", [P, 2, D])
        x1b = sb("x1b", [P, 2, D])
        zb = sb("zb", [P, 2, D])
        logits = sb("logits", [P, 2, EXPERTS])
        top8 = sb("top8", [P, 2, 8])
        idx8 = sb("idx8", [P, 2, 8], U32)
        idxf = sb("idxf", [P, 2, 2])
        vals = sb("vals", [P, NT, 2])
        gate = sb("gate", [P, NT, 2])
        chosen = sb("chosen", [P, NT, EXPERTS], BF16)
        slots_f = sb("slots_f", [P, NT, 2])
        slots = sb("slots", [P, NT, 2], I32)
        eend = sb("eend", [P, EXPERTS])
        etile = sb("etile", [P, EXPERTS])
        etile_i = sb("etile_i", [P, EXPERTS], I32)
        ebase = sb("ebase", [P, EXPERTS])
        tile_expert = sb("tile_expert", [1, ET], I32)
        dn = sb("dn", [P, NT])
        den = sb("den", [P, NT])
        slot_st = sb("slot_st", [P, 2, 2], I32)

        bank = [ctx.enter_context(nc.psum_tensor(f"bank{i}", [P, 512], F32)) for i in range(8)]
        NG = GRP * BINS
        assert NG <= 512

        def counts(b):
            return bank[b][:, 0:NG].rearrange("p (c b) -> p c b", c=GRP)

        s_src, s_edge, s_par = sem("s_src"), sem("s_edge"), sem("s_par")
        s_const, s_made, s_recs = sem("s_const"), sem("s_made"), sem("s_recs")
        s_fill, s_zero, s_zeroed = sem("s_fill"), sem("s_zero"), sem("s_zeroed")
        s_hot, s_hist = sem("s_hot"), sem("s_hist")
        s_mid, s_base, s_based, s_colT, s_ends, s_tbl = (sem(n) for n in (
            "s_mid", "s_base", "s_based", "s_colT", "s_ends", "s_tbl"))
        s_rank, s_read, s_count, s_red, s_pos = (sem(n) for n in (
            "s_rank", "s_read", "s_count", "s_red", "s_pos"))
        s_scat = sem2("s_scat")
        s_xin, s_ln_dve, s_ln_act, s_ln_pe, s_hst = (sem2(n) for n in (
            "s_xin", "s_ln_dve", "s_ln_act", "s_ln_pe", "s_hst"))
        s_recin = sem2("s_recin")
        s_row = [sem(f"s_row{k}") for k in range(PER)]
        s_pick, s_sum, s_acc = sem("s_pick"), sem("s_sum"), sem("s_acc")
        s_rt_x, s_rt_dve, s_rt_act, s_rt_pe, s_x1st = (sem2(n) for n in (
            "s_rt_x", "s_rt_dve", "s_rt_act", "s_rt_pe", "s_x1st"))
        s_ch, s_chp, s_m2, s_exp, s_ec, s_ecs, s_past, s_etp = (sem(n) for n in (
            "s_ch", "s_chp", "s_m2", "s_exp", "s_ec", "s_ecs", "s_past", "s_etp"))
        s_slots, s_etab = sem("s_slots"), sem("s_etab")
        s_st_act, s_st_dve, s_disp = sem2("s_st_act"), sem2("s_st_dve"), sem2("s_disp")
        s_w, s_exin, s_ex_pe, s_ex_act, s_ex_dve, s_exst = (
            sem("s_w"), sem2("s_exin"), sem2("s_ex_pe"), sem2("s_ex_act"), sem2("s_ex_dve"), sem2("s_exst"))
        s_cx, s_cidx, s_cg, s_cdve, s_out = (sem2(n) for n in (
            "s_cx", "s_cidx", "s_cg", "s_cdve", "s_out"))
        s_gate, s_cleared = sem("s_gate"), sem("s_cleared")
        s_held = {n: sem(f"s_held_{n}") for n in ("pool", "act", "dve")}

        def held(eng, which, s, value):
            eng.wait_ge(s, value)
            eng.sem_inc(s_held[which], 1)

        x_rows = x
        NP_ = NT // 2
        assert NT % 2 == 0 and STEPS % 2 == 0 and ET % 2 == 0

        block = ctx.enter_context(nc.Block())

        @block.sync
        def _(sp):
            def spread(ap, dst_sb, s):
                full = (P - 1) * COLS
                sp.dma_start(dst_sb[0:P - 1, :], ap[0:full].rearrange("(p t) -> p t", t=COLS)).then_inc(s, 16)
                sp.dma_start(dst_sb[P - 1:P, 0:LAST], ap[full:EDGES].rearrange("(p t) -> p t", p=1)).then_inc(s, 16)

            sp.wait_ge(s_made, 3)
            spread(src, src_sb, s_src)
            spread(dst, dst_sb, s_edge)
            spread(edge_weight, ew_sb, s_edge)
            sp.dma_start(gw_sb[:, :, :], gw.rearrange("(k p) n -> p k n", p=P)).then_inc(s_par, 16)
            sp.dma_start(wr_sb[:, :, :], wr.rearrange("(k p) n -> p k n", p=P)).then_inc(s_par, 16)
            for ap, t in ((gb, gb_sb), (gamma, gamma_sb), (beta, beta_sb), (br, br_sb)):
                sp.dma_start(t[:, :], ap.partition_broadcast(P)).then_inc(s_par, 16)
            sp.wait_ge(s_zero, 2)
            part = SLOTT // FILLS
            grid = edges_sorted.rearrange("(p t) w -> p t w", p=P)
            for k in range(FILLS):
                sp.dma_start(grid[:, k * part:(k + 1) * part, :], fill[:, :, :]).then_inc(s_fill, 16)
            zgrid = expert_in.rearrange("(p t) d -> p (t d)", p=P)
            for k in range(ET // ZROWS):
                sp.dma_start(zgrid[:, k * ZROWS * D:(k + 1) * ZROWS * D], zeros[:, :]).then_inc(s_zeroed, 16)

            def node_tile(i):
                for sub in range(2):
                    t = 2 * i + sub
                    n = TAIL if is_last(i, NP_) and sub else P
                    if not is_first(i):
                        sp.wait_ge(s_ln_dve[sub], done(LN_DVE, "norm", i - 1))
                    sp.dma_start(xin[0:n, sub, :], x_rows[bass.ds(t * P, n), :]).then_inc(s_xin[sub], 16)
                for sub in range(2):
                    t = 2 * i + sub
                    sp.wait_ge(s_ln_act[sub], done(LN_ACT, "h", i))
                    sp.dma_start(h_rows[bass.ds(t * P, P), :], h_out[:, sub, :]).then_inc(s_hst[sub], 16)

            rounds(sp, NP_, node_tile)

            for sub in range(2):
                sp.wait_ge(s_scat[sub], 16 * PER * NP_)

            def sorted_step(i):
                for sub in range(2):
                    step = 2 * i + sub
                    if not is_first(i):
                        sp.wait_ge(s_sum, PER * (step - 1))
                    sp.dma_start(rec_in[:, sub, :, :],
                                 grid[:, bass.ds(step * PER, PER), :]).then_inc(s_recin[sub], 16)

            rounds(sp, STEPS // 2, sorted_step)

            def router_tile(i):
                for sub in range(2):
                    t = 2 * i + sub
                    n = TAIL if is_last(i, NP_) and sub else P
                    if is_first(i):
                        sp.wait_ge(s_ln_dve[sub], done(LN_DVE, "norm", NP_ - 1))
                    else:
                        sp.wait_ge(s_rt_dve[sub], done(RT_DVE, "xa", i - 1))
                    sp.dma_start(xin[0:n, sub, :], x_rows[bass.ds(t * P, n), :]).then_inc(s_rt_x[sub], 16)
                for sub in range(2):
                    t = 2 * i + sub
                    sp.wait_ge(s_rt_dve[sub], done(RT_DVE, "x1", i))
                    sp.dma_start(x1_rows[bass.ds(t * P, P), :], x1b[:, sub, :]).then_inc(s_x1st[sub], 16)

            rounds(sp, NP_, router_tile)

            for sub in range(2):
                sp.wait_ge(s_disp[sub], 32 * NP_)
            for e in range(EXPERTS):
                sp.dma_start(w1_sb[:, e], w1[e].rearrange("(k p) n -> p k n", p=P)).then_inc(s_w, 16)
                sp.dma_start(w2_sb[:, e], w2[e].rearrange("(k p) n -> p k n", p=P)).then_inc(s_w, 16)
            sp.dma_start(b1_sb, b1.partition_broadcast(P)).then_inc(s_w, 16)
            sp.dma_start(b2_sb, b2.partition_broadcast(P)).then_inc(s_w, 16)

            def expert_tile(i):
                for sub in range(2):
                    t = 2 * i + sub
                    if is_first(i):
                        sp.wait_ge(s_rt_dve[sub], done(RT_DVE, "vals", NP_ - 1))
                    else:
                        sp.wait_ge(s_ex_pe[sub], done(EX_PE, "xT", i - 1))
                    sp.dma_start(xin[:, sub, :], expert_in[bass.ds(t * P, P), :]).then_inc(s_exin[sub], 16)
                for sub in range(2):
                    t = 2 * i + sub
                    sp.wait_ge(s_ex_dve[sub], done(EX_DVE, "b2", i))
                    sp.dma_start(expert_out[bass.ds(t * P, P), :], ex_y[:, sub, :]).then_inc(s_exst[sub], 16)

            rounds(sp, ET // 2, expert_tile)

            def combine_tile(i):
                for sub in range(2):
                    t = 2 * i + sub
                    if is_first(i):
                        sp.wait_ge(s_x1st[sub], 16 * NP_)
                    else:
                        sp.wait_ge(s_cdve[sub], 2 * i)
                    sp.dma_start(x1b[:, sub, :], x1_rows[bass.ds(t * P, P), :]).then_inc(s_cx[sub], 16)
                for sub in range(2):
                    t = 2 * i + sub
                    n = TAIL if is_last(i, NP_) and sub else P
                    sp.wait_ge(s_cdve[sub], 2 * (i + 1))
                    sp.dma_start(out[bass.ds(t * P, n), :], zb[0:n, sub, :]).then_inc(s_out[sub], 16)

            rounds(sp, NP_, combine_tile)
            for sub in range(2):
                sp.wait_ge(s_out[sub], 16 * NP_)

        @block.gpsimd
        def _(pool):
            g = nc.gpsimd
            g.iota(ramp_i, [[1, SLOTT]], base=0, channel_multiplier=0).then_inc(s_const, 1)
            g.memset(tri[:, :], 1.0).then_inc(s_const, 1)
            g.memset(rest[:, :], 1.0).then_inc(s_const, 1)
            g.memset(ident[:, :], 0.0).then_inc(s_const, 1)
            g.memset(valid[:, :], 1.0).then_inc(s_const, 1)
            pool.wait_ge(s_const, 5)
            g.affine_select(out=tri[:, :], in_=tri[:, :], compare_op=ALU.is_gt, fill=0.0, base=0,
                            pattern=[[1, P]], channel_multiplier=-1).then_inc(s_const, 1)
            g.affine_select(out=rest[:, :], in_=rest[:, :], compare_op=ALU.is_ge, fill=0.0, base=0,
                            pattern=[[-1, P]], channel_multiplier=1).then_inc(s_const, 1)
            g.affine_select(out=ident[:, :], in_=ident[:, :], compare_op=ALU.not_equal, fill=1.0, base=0,
                            pattern=[[-1, P]], channel_multiplier=1).then_inc(s_const, 1)
            g.affine_select(out=valid[:, :], in_=valid[:, :], compare_op=ALU.is_ge, fill=0.0, base=TAIL - 1,
                            pattern=[[0, 1]], channel_multiplier=-1).then_inc(s_const, 1)
            g.memset(zeros[:, :], 0.0).then_inc(s_zero, 1)

            pool.wait_ge(s_fill, 16 * FILLS)

            def scatter_step(i):
                for sub in range(2):
                    held(pool, "pool", s_pos, done(POS, "rec", 2 * i + sub))
                    for k in range(PER):
                        pool.indirect_dma_start(
                            out=edges_sorted[:, :],
                            out_offset=bass.IndirectOffsetOnAxis(ap=addr[:, sub, k:k + 1], axis=0),
                            in_=rec_out[:, sub, k, :], in_offset=None,
                            bounds_check=NSLOT - 1, oob_is_err=False).then_inc(s_scat[sub], 16)

            rounds(pool, NP_, scatter_step)

            pool.wait_ge(s_cleared, 2)
            for sub in range(2):
                pool.wait_ge(s_hst[sub], 16 * NP_)

            def gather_step(i):
                for sub in range(2):
                    step = 2 * i + sub
                    held(pool, "pool", s_recin[sub], 16 * (i + 1))
                    for k in range(PER):
                        if k % 4 == 0 and not (is_first(i) and sub == 0):
                            held(pool, "pool", s_sum, PER * step - PER + k + 4)
                        pool.indirect_dma_start(
                            out=rows[:, k, :], out_offset=None, in_=h_rows[:, :],
                            in_offset=bass.IndirectOffsetOnAxis(ap=rec_in[:, sub, k, 0:1], axis=0),
                            bounds_check=NODES - 1, oob_is_err=False).then_inc(s_row[k], 16)

            rounds(pool, STEPS // 2, gather_step)

            pool.wait_ge(s_zeroed, 16 * (ET // ZROWS))

            def dispatch_tile(i):
                for sub in range(2):
                    n = TAIL if is_last(i, NP_) and sub else P
                    held(pool, "pool", s_st_act[sub], i + 1)
                    held(pool, "pool", s_st_dve[sub], i + 1)
                    for c in range(2):
                        pool.indirect_dma_start(
                            out=expert_in[:, :],
                            out_offset=bass.IndirectOffsetOnAxis(ap=slot_st[0:n, sub, c:c + 1], axis=0),
                            in_=normed[0:n, sub, :], in_offset=None,
                            bounds_check=ET * P - 1, oob_is_err=False).then_inc(s_disp[sub], 16)

            rounds(pool, NP_, dispatch_tile)

            for sub in range(2):
                pool.wait_ge(s_exst[sub], 16 * (ET // 2))

            def fetch_tile(i):
                for sub in range(2):
                    n = TAIL if is_last(i, NP_) and sub else P
                    held(pool, "pool", s_cidx[sub], i + 1)
                    for c, y in enumerate((ya1, ya2)):
                        pool.indirect_dma_start(
                            out=y[0:n, sub, :], out_offset=None, in_=expert_out[:, :],
                            in_offset=bass.IndirectOffsetOnAxis(ap=slot_st[0:n, sub, c:c + 1], axis=0),
                            bounds_check=ET * P - 1, oob_is_err=False).then_inc(s_cg[sub], 16)

            rounds(pool, NP_, fetch_tile)

        @block.tensor
        def _(pe):
            mm = nc.tensor.matmul
            pe.wait_ge(s_made, 7)
            pe.wait_ge(s_const, 9)

            def hist_step(t):
                for gidx in range(GRPS):
                    pe.wait_ge(s_hot, GRPS * t + gidx + 1)
                    mm(counts(gidx % 2), ones[:, :], hot[:, gidx, :, :], start=is_first(t) and gidx < 2,
                       stop=is_last(t, NT) and gidx >= GRPS - 2, skip_group_check=True).then_inc(s_hist, 1)

            rounds(pe, NT, hist_step)

            pe.wait_ge(s_ends, 1)
            mm(bank[2][0:NT, 0:1], binend[0:1, 0:NT], onesf[0:1, 0:1], start=True, stop=True).then_inc(s_colT, 1)
            pe.wait_ge(s_base, 1)
            for b in range(2):
                mm(counts(b), onesf[0:1, :], base[0:1, GRP * b:GRP * b + GRP, :], start=True, stop=False,
                   skip_group_check=True).then_inc(s_based, 1)
            pe.wait_ge(s_past, 1)
            quarter = SLOTT // 4
            for q in range(4):
                mm(bank[3 + q][0:1, 0:quarter], ones[0:NT, 0:1], past[0:NT, q * quarter:(q + 1) * quarter],
                   start=True, stop=True).then_inc(s_tbl, 1)
            pe.wait_ge(s_tbl, 8)

            def rank(t, gidx):
                pe.wait_ge(s_hot, GRPS * NT + GRPS * t + gidx + 1)
                mm(counts(gidx % 2), tri[:, :], hot[:, gidx, :, :], start=False, stop=False,
                   skip_group_check=True).then_inc(s_rank, 1)

            def count(t, gidx):
                pe.wait_ge(s_read, GRPS * t + gidx + 1)
                mm(counts(gidx % 2), rest[:, :], hot[:, gidx, :, :], start=False, stop=False,
                   skip_group_check=True).then_inc(s_count, 1)

            def ln_T(i, sub):
                pe.wait_ge(s_ln_dve[sub], done(LN_DVE, "norm", i))
                for k in range(KD):
                    last = nc.tensor.transpose(bank[2 + sub][:, k * P:(k + 1) * P],
                                               normed[:, sub, k * P:(k + 1) * P], ident[:, :])
                last.then_inc(s_ln_pe[sub], 1)

            def ln_h(i, sub):
                pe.wait_ge(s_ln_act[sub], done(LN_ACT, "nT", i))
                for k in range(KD):
                    last = mm(bank[4 + sub][:, 0:D], normedT[:, sub, k * P:(k + 1) * P], gw_sb[:, k, :],
                              start=(k == 0), stop=(k == KD - 1))
                last.then_inc(s_ln_pe[sub], 1)

            pe.wait_ge(s_par, 16 * 6)

            def sort_step(i):
                for sub in range(2):
                    t = 2 * i + sub
                    rank(t, 0)
                    rank(t, 1)
                    count(t, 0)
                    rank(t, 2)
                    count(t, 1)
                    rank(t, 3)
                    count(t, 2)
                    count(t, 3)
                    if sub == 0:
                        ln_T(i, 0)
                ln_h(i, 0)
                ln_T(i, 1)
                ln_h(i, 1)

            rounds(pe, NP_, sort_step)

            for sub in range(2):
                pe.wait_ge(s_ln_act[sub], done(LN_ACT, "h", NP_ - 1))

            def sum_step(i):
                for sub in range(2):
                    for k in range(PER):
                        n = PER * (2 * i + sub) + k
                        pe.wait_ge(s_pick, n + 1)
                        pe.wait_ge(s_row[k], 16 * (2 * i + sub + 1))
                        if not (is_first(i) and sub == 0 and k < 4):
                            pe.wait_ge(s_acc, n - 3)
                        mm(bank[k % 4][:, 0:D], pick[:, k % 4, :], rows[:, k, :],
                           start=True, stop=True).then_inc(s_sum, 1)

            rounds(pe, STEPS // 2, sum_step)

            def router_tile(i):
                for sub in range(2):
                    pe.wait_ge(s_rt_dve[sub], done(RT_DVE, "xn", i))
                    if is_first(i):
                        pe.wait_ge(s_acc, SLOTT)
                    for k in range(KD):
                        last = nc.tensor.transpose(bank[2 + sub][:, k * P:(k + 1) * P],
                                                   normed[:, sub, k * P:(k + 1) * P], ident[:, :])
                    last.then_inc(s_rt_pe[sub], 1)
                for sub in range(2):
                    pe.wait_ge(s_rt_act[sub], done(RT_ACT, "xT", i))
                    for k in range(KD):
                        last = mm(bank[4 + sub][:, 0:EXPERTS], normedT[:, sub, k * P:(k + 1) * P],
                                  wr_sb[:, k, :], start=(k == 0), stop=(k == KD - 1))
                    last.then_inc(s_rt_pe[sub], 1)

            rounds(pe, NP_, router_tile)

            half = NT // 2 * EXPERTS
            ch = chosen[:, :, :].rearrange("p t e -> p (t e)")
            pe.wait_ge(s_ch, 1)
            for q in range(2):
                mm(bank[q][:, 0:half], tri[:, :], ch[:, q * half:(q + 1) * half], start=True, stop=True)
            for q in range(2):
                last = mm(bank[2 + q][:, 0:half], ones[:, :], ch[:, q * half:(q + 1) * half], start=True, stop=True)
            last.then_inc(s_chp, 1)
            pe.wait_ge(s_ec, 1)
            mm(bank[6][0:EXPERTS, 0:1], eend[0:1, 0:EXPERTS], onesf[0:1, 0:1], start=True, stop=True).then_inc(s_ecs, 1)
            pe.wait_ge(s_etp, 1)
            mm(bank[7][0:1, 0:ET], ones[0:EXPERTS, 0:1], past[0:EXPERTS, 0:ET], start=True, stop=True).then_inc(s_ecs, 1)

            pe.wait_ge(s_w, 16 * (2 * EXPERTS + 2))
            pe.wait_ge(s_etab, 1)

            def expert_tile(i):
                exp = [pe.value_load(tile_expert[0:1, bass.ds(2 * i + sub, 1)], min_val=0, max_val=EXPERTS - 1)
                       for sub in range(2)]
                for sub in range(2):
                    b = 4 * sub
                    pe.wait_ge(s_exin[sub], 16 * (i + 1))
                    for k in range(KD):
                        last = nc.tensor.transpose(bank[b][:, k * P:(k + 1) * P],
                                                   xin[:, sub, k * P:(k + 1) * P], ident[:, :])
                    last.then_inc(s_ex_pe[sub], 1)
                for sub in range(2):
                    b = 4 * sub
                    pe.wait_ge(s_ex_act[sub], done(EX_ACT, "xT", i))
                    for k in range(KD):
                        last = mm(bank[b + 1][:, 0:HID], normedT[:, sub, k * P:(k + 1) * P],
                                  w1_sb[:, bass.ds(exp[sub], 1), k, :].rearrange("p a n -> p (a n)"),
                                  start=(k == 0), stop=(k == KD - 1))
                    last.then_inc(s_ex_pe[sub], 1)
                for sub in range(2):
                    b = 4 * sub
                    pe.wait_ge(s_ex_act[sub], done(EX_ACT, "gelu", i))
                    for k in range(KH):
                        last = nc.tensor.transpose(bank[b + 2][:, k * P:(k + 1) * P],
                                                   ex_h[:, sub, k * P:(k + 1) * P], ident[:, :])
                    last.then_inc(s_ex_pe[sub], 1)
                for sub in range(2):
                    b = 4 * sub
                    pe.wait_ge(s_ex_dve[sub], done(EX_DVE, "hT", i))
                    for k in range(KH):
                        last = mm(bank[b + 3][:, 0:D], ex_hT[:, sub, k * P:(k + 1) * P],
                                  w2_sb[:, bass.ds(exp[sub], 1), k, :].rearrange("p a n -> p (a n)"),
                                  start=(k == 0), stop=(k == KH - 1))
                    last.then_inc(s_ex_pe[sub], 1)

            rounds(pe, ET // 2, expert_tile)

        @block.scalar
        def _(act):
            a = nc.scalar
            act.wait_ge(s_made, 7)

            def std_of(sub, s, wait_sem, value):
                act.wait_ge(wait_sem, value)
                a.activation(std[:, sub, :], mv[:, sub, 1:2], ACT.Sqrt, bias=eps[:, 0:1]).then_inc(s, 1)

            def ln_tile(i):
                def take_T(sub):
                    act.wait_ge(s_ln_pe[sub], done(LN_PE, "nT", i))
                    a.copy(normedT[:, sub, :], bank[2 + sub][:, 0:D]).then_inc(s_ln_act[sub], 1)

                def take_h(sub):
                    if not is_first(i):
                        act.wait_ge(s_hst[sub], 16 * i)
                    act.wait_ge(s_ln_pe[sub], done(LN_PE, "h", i))
                    a.copy(h_out[:, sub, :], bank[4 + sub][:, 0:D]).then_inc(s_ln_act[sub], 1)

                std_of(0, s_ln_act[0], s_ln_dve[0], done(LN_DVE, "aggr", i))
                take_T(0)
                std_of(1, s_ln_act[1], s_ln_dve[1], done(LN_DVE, "aggr", i))
                take_h(0)
                take_T(1)
                take_h(1)

            rounds(act, NP_, ln_tile)

            def router_tile(i):
                for sub in range(2):
                    std_of(sub, s_rt_act[sub], s_rt_dve[sub], done(RT_DVE, "aggr1", i))
                for sub in range(2):
                    std_of(sub, s_rt_act[sub], s_rt_dve[sub], done(RT_DVE, "aggr2", i))
                for sub in range(2):
                    held(act, "act", s_rt_dve[sub], done(RT_DVE, "xn", i))
                    a.copy(acc[:, bass.ds(2 * i + sub, 1), :].rearrange("p a d -> p (a d)"),
                           normed[:, sub, :]).then_inc(s_rt_act[sub], 1)
                    act.wait_ge(s_rt_pe[sub], done(RT_PE, "xT", i))
                    a.copy(normedT[:, sub, :], bank[2 + sub][:, 0:D]).then_inc(s_rt_act[sub], 1)

            rounds(act, NP_, router_tile)

            act.wait_ge(s_exp, 1)
            a.activation(den[:, :], dn[:, :], ACT.Exp).then_inc(s_exp, 1)

            def stage_tile(i):
                for sub in range(2):
                    if is_first(i):
                        act.wait_ge(s_rt_pe[sub], done(RT_PE, "logits", NP_ - 1))
                        act.wait_ge(s_rt_act[sub], done(RT_ACT, "xT", NP_ - 1))
                    else:
                        held(act, "act", s_disp[sub], 32 * i)
                    a.copy(normed[:, sub, :], acc[:, bass.ds(2 * i + sub, 1), :].rearrange("p a d -> p (a d)"))\
                        .then_inc(s_st_act[sub], 1)

            rounds(act, NP_, stage_tile)

            def expert_tile(i):
                for sub in range(2):
                    act.wait_ge(s_ex_pe[sub], done(EX_PE, "xT", i))
                    a.copy(normedT[:, sub, :], bank[4 * sub][:, 0:D]).then_inc(s_ex_act[sub], 1)
                for sub in range(2):
                    act.wait_ge(s_ex_dve[sub], done(EX_DVE, "b1", i))
                    a.activation(ex_h[:, sub, :], ex_u[:, sub, :], ACT.Gelu).then_inc(s_ex_act[sub], 1)

            rounds(act, ET // 2, expert_tile)

        @block.vector
        def _(dve):
            v = nc.vector
            link_count = [0]

            def link(ins, s=s_mid):
                link_count[0] += 1
                ins.then_inc(s, 1)
                dve.wait_ge(s, link_count[0])

            v.memset(src_sb[:, :], NT * P).then_inc(s_made, 1)
            v.memset(dst_sb[:, :], 0).then_inc(s_made, 1)
            v.memset(ew_sb[:, :], 0.0).then_inc(s_made, 1)
            v.memset(ones[:, :], 1.0).then_inc(s_made, 1)
            v.memset(onesf[:, :], 1.0).then_inc(s_made, 1)
            v.memset(eps[:, :], EPS).then_inc(s_made, 1)
            v.memset(xin[:, :, :], 0.0).then_inc(s_made, 1)
            link(v.memset(fill[:, :, :], 0))
            v.memset(fill_f[:, :, 1], 2.0 * P)
            v.memset(fill[:, :, 0], FAR).then_inc(s_zero, 1)
            dve.wait_ge(s_const, 1)
            link(v.tensor_copy(ramp[:, :], ramp_i))
            dve.wait_ge(s_src, 32)
            link(v.tensor_scalar(ramp_i[:, 0:COLS], src_sb[:, :], 7, None, ALU.arith_shift_right))
            v.tensor_copy(binf, ramp_i[:, 0:COLS]).then_inc(s_recs, 1)
            link(v.tensor_scalar(src_sb[:, :], src_sb[:, :], P - 1, None, ALU.bitwise_and))
            v.tensor_copy(recs_f[:, :, 1], src_sb[:, :]).then_inc(s_recs, 1)
            dve.wait_ge(s_edge, 64)
            v.tensor_copy(recs[:, :, 0], dst_sb[:, :]).then_inc(s_recs, 1)
            v.tensor_copy(recs_f[:, :, 2], ew_sb[:, :]).then_inc(s_recs, 1)
            dve.wait_ge(s_recs, 4)
            v.memset(acc[:, :, :], 0.0).then_inc(s_cleared, 1)

            numbers = ramp[:, 0:BINS].unsqueeze(1).broadcast_to([P, GRP, BINS])

            def one_hot(t, gidx):
                cols = binf[:, bass.ds(PER * t + GRP * gidx, GRP)].unsqueeze(2).broadcast_to([P, GRP, BINS])
                v.tensor_tensor(hot[:, gidx, :, :], numbers, cols, ALU.is_equal).then_inc(s_hot, 1)

            def hist_step(t):
                for gidx in range(GRPS):
                    if not is_first(t):
                        dve.wait_ge(s_hist, GRPS * t - GRPS + gidx + 1)
                    one_hot(t, gidx)

            rounds(dve, NT, hist_step)

            dve.wait_ge(s_hist, GRPS * NT)
            for b in range(2):
                link(v.tensor_copy(totals[:, GRP * b:GRP * b + GRP, :], counts(b)))
            link(v.tensor_reduce(binsum[:, :], totals[:, :, :].rearrange("p c b -> p b c"), AX_X, ALU.add))
            link(v.tensor_scalar(binsum[:, :], binsum[:, :], float(P - 1), None, ALU.add))
            link(v.tensor_copy(bintile_i[:, :], binsum[:, :]))
            link(v.tensor_scalar(bintile_i[:, :], bintile_i[:, :], 7, None, ALU.arith_shift_right))
            link(v.tensor_copy(bintile[:, :], bintile_i[:, :]))
            link(v.tensor_tensor_scan(binend[:, :], onesf[:, 0:BINS], bintile[:, :], 0.0, ALU.mult, ALU.add))
            v.sem_inc(s_ends, 1)
            link(v.tensor_tensor(binsum[:, :], binend[:, :], bintile[:, :], ALU.subtract))
            link(v.tensor_scalar(base[:, 0, :], binsum[:, :], float(P), None, ALU.mult))
            for c in range(1, CHAINS):
                link(v.tensor_tensor(base[:, c, :], base[:, c - 1, :], totals[:, c - 1, :], ALU.add))
            link(v.memset(base[:, :, NT:BINS], BEYOND))
            v.sem_inc(s_base, 1)
            dve.wait_ge(s_colT, 1)
            link(v.tensor_copy(endcol[0:NT, :], bank[2][0:NT, 0:1]))
            v.tensor_scalar(past[0:NT, :], ramp[0:NT, :], endcol[0:NT, 0:1], None, ALU.is_ge).then_inc(s_past, 1)
            quarter = SLOTT // 4
            for q in range(4):
                dve.wait_ge(s_tbl, 4)
                v.tensor_scalar(tile_bin[0:1, q * quarter:(q + 1) * quarter], bank[3 + q][0:1, 0:quarter],
                                float(NT - 1), None, ALU.min).then_inc(s_tbl, 1)
            dve.wait_ge(s_based, 2)
            v.memset(rows[:, :, :], 0.0).then_inc(s_cleared, 1)

            def positions(i, sub):
                t = 2 * i + sub
                dve.wait_ge(s_red, GRPS * t + GRPS)
                v.tensor_copy(pos_i[:, sub, :], pos[:, sub, :]).then_inc(s_pos, 1)
                dve.wait_ge(s_pos, done(POS, "int", t))
                v.tensor_scalar(pos_row[:, sub, :], pos_i[:, sub, :], P - 1, None, ALU.bitwise_and).then_inc(s_pos, 1)
                v.tensor_scalar(pos_col[:, sub, :], pos_i[:, sub, :], 7, None, ALU.arith_shift_right).then_inc(s_pos, 1)
                dve.wait_ge(s_pos, done(POS, "col", t))
                if not is_first(i):
                    dve.wait_ge(s_scat[sub], 16 * PER * i)
                v.scalar_tensor_tensor(out=addr[:, sub, :], in0=pos_row[:, sub, :], scalar=float(SLOTT),
                                       in1=pos_col[:, sub, :], op0=ALU.mult, op1=ALU.add).then_inc(s_pos, 1)
                v.tensor_copy(rec_out[:, sub, :, :], recs[:, bass.ds(PER * t, PER), :]).then_inc(s_pos, 1)

            def held_aggr(s, sub, value):
                held(dve, "dve", s, value)
                v.bn_aggr(mv[:, sub, :], stats[:, sub, :]).then_inc(s, 1)

            def sort_step(i):
                for sub in range(2):
                    t = 2 * i + sub
                    s = s_ln_dve[sub]

                    def hot_one(gidx):
                        if not is_first(t):
                            dve.wait_ge(s_count, GRPS * t - GRPS + gidx + 1)
                        one_hot(t, gidx)

                    def extract(gidx):
                        dve.wait_ge(s_rank, GRPS * t + gidx + 1)
                        v.tensor_tensor(prod[:, gidx % 2, :, :], hot[:, gidx, :, :], counts(gidx % 2),
                                        ALU.mult).then_inc(s_read, 1)
                        dve.wait_ge(s_read, GRPS * t + gidx + 1)
                        v.tensor_reduce(pos[:, sub, GRP * gidx:GRP * gidx + GRP], prod[:, gidx % 2, :, :],
                                        AX_X, ALU.add).then_inc(s_red, 1)

                    hot_one(0)
                    hot_one(1)
                    dve.wait_ge(s_xin[sub], 16 * (i + 1))
                    v.bn_stats(stats[:, sub, :], xin[:, sub, :]).then_inc(s, 1)
                    extract(0)
                    held_aggr(s, sub, done(LN_DVE, "stats", i))
                    hot_one(2)
                    extract(1)
                    hot_one(3)
                    extract(2)
                    dve.wait_ge(s_ln_act[sub], done(LN_ACT, "std", i))
                    v.reciprocal(rstd[:, sub, :], std[:, sub, :]).then_inc(s, 1)
                    extract(3)
                    dve.wait_ge(s, done(LN_DVE, "rstd", i))
                    if not is_first(i):
                        dve.wait_ge(s_ln_pe[sub], done(LN_PE, "nT", i - 1))
                    v.tensor_scalar(normed[:, sub, :], xin[:, sub, :], mv[:, sub, 0:1], rstd[:, sub, 0:1],
                                    ALU.subtract, ALU.mult).then_inc(s, 1)
                    positions(i, sub)

            rounds(dve, NP_, sort_step)

            def make_pick(i, sub, k):
                n = PER * (2 * i + sub) + k
                if k == 0:
                    dve.wait_ge(s_recin[sub], 16 * (i + 1))
                if not (is_first(i) and sub == 0 and k < 4):
                    dve.wait_ge(s_sum, n - 3)
                v.tensor_scalar(pick[:, k % 4, :], ramp[:, 0:P], rec_in_f[:, sub, k, 1:2],
                                rec_in_f[:, sub, k, 2:3], ALU.is_equal, ALU.mult).then_inc(s_pick, 1)

            def add_sum(i, sub, k, where):
                n = PER * (2 * i + sub) + k
                place = acc[:, bass.ds(where, 1), :].rearrange("p a d -> p (a d)")
                dve.wait_ge(s_sum, n + 1)
                if not (is_first(i) and sub == 0 and k == 0):
                    dve.wait_ge(s_acc, n)
                v.tensor_tensor(place, place, bank[k % 4][:, 0:D], ALU.add).then_inc(s_acc, 1)

            def sum_step(i):
                for sub in range(2):
                    make_pick(i, sub, 0)
                    make_pick(i, sub, 1)
                    for k in range(PER):
                        if k + 2 < PER:
                            make_pick(i, sub, k + 2)
                        where = dve.value_load(tile_bin[0:1, bass.ds(PER * (2 * i + sub) + k, 1)],
                                               min_val=0, max_val=NT - 1)
                        add_sum(i, sub, k, where)

            dve.wait_ge(s_tbl, 8)
            dve.wait_ge(s_cleared, 2)
            rounds(dve, STEPS // 2, sum_step)

            dve.wait_ge(s_acc, SLOTT)

            def router_tile(i):
                S = s_rt_dve

                def at(name):
                    return done(RT_DVE, name, i)

                for sub in range(2):
                    place = acc[:, bass.ds(2 * i + sub, 1), :].rearrange("p a d -> p (a d)")
                    dve.wait_ge(s_rt_x[sub], 16 * (i + 1))
                    v.tensor_tensor(ya[:, sub, :], xin[:, sub, :], place, ALU.add).then_inc(S[sub], 1)
                for sub in range(2):
                    dve.wait_ge(S[sub], at("xa"))
                    if not is_first(i):
                        dve.wait_ge(s_x1st[sub], 16 * i)
                    v.tensor_tensor(x1b[:, sub, :], ya[:, sub, :], gb_sb[:, :], ALU.add).then_inc(S[sub], 1)
                for sub in range(2):
                    dve.wait_ge(S[sub], at("x1"))
                    v.bn_stats(stats[:, sub, :], x1b[:, sub, :]).then_inc(S[sub], 1)
                for sub in range(2):
                    held_aggr(S[sub], sub, at("stats1"))
                for sub in range(2):
                    dve.wait_ge(s_rt_act[sub], done(RT_ACT, "std1", i))
                    v.reciprocal(rstd[:, sub, :], std[:, sub, :]).then_inc(S[sub], 1)
                for sub in range(2):
                    dve.wait_ge(S[sub], at("rstd1"))
                    v.tensor_scalar(ya[:, sub, :], x1b[:, sub, :], mv[:, sub, 0:1], rstd[:, sub, 0:1],
                                    ALU.subtract, ALU.mult).then_inc(S[sub], 1)
                for sub in range(2):
                    dve.wait_ge(S[sub], at("y"))
                    v.bn_stats(stats[:, sub, :], ya[:, sub, :]).then_inc(S[sub], 1)
                for sub in range(2):
                    held_aggr(S[sub], sub, at("stats2"))
                for sub in range(2):
                    dve.wait_ge(s_rt_act[sub], done(RT_ACT, "std2", i))
                    v.reciprocal(rstd[:, sub, :], std[:, sub, :]).then_inc(S[sub], 1)
                for sub in range(2):
                    dve.wait_ge(S[sub], at("rstd2"))
                    v.tensor_scalar(zb[:, sub, :], ya[:, sub, :], mv[:, sub, 0:1], rstd[:, sub, 0:1],
                                    ALU.subtract, ALU.mult).then_inc(S[sub], 1)
                for sub in range(2):
                    dve.wait_ge(S[sub], at("z"))
                    v.tensor_tensor(zb[:, sub, :], zb[:, sub, :], gamma_sb[:, :], ALU.mult).then_inc(S[sub], 1)
                for sub in range(2):
                    dve.wait_ge(S[sub], at("zg"))
                    if not is_first(i):
                        dve.wait_ge(s_rt_act[sub], done(RT_ACT, "xT", i - 1))
                    v.tensor_tensor(normed[:, sub, :], zb[:, sub, :], beta_sb[:, :], ALU.add).then_inc(S[sub], 1)
                for sub in range(2):
                    dve.wait_ge(s_rt_pe[sub], done(RT_PE, "logits", i))
                    v.tensor_tensor(logits[:, sub, :], bank[4 + sub][:, 0:EXPERTS], br_sb[:, :], ALU.add)\
                        .then_inc(S[sub], 1)
                for sub in range(2):
                    held(dve, "dve", S[sub], at("logits"))
                    v.max(top8[:, sub, :], logits[:, sub, :]).then_inc(S[sub], 1)
                for sub in range(2):
                    held(dve, "dve", S[sub], at("top"))
                    v.max_index(idx8[:, sub, :], top8[:, sub, :], logits[:, sub, :]).then_inc(S[sub], 1)
                for sub in range(2):
                    dve.wait_ge(S[sub], at("index"))
                    v.tensor_copy(idxf[:, sub, :], idx8[:, sub, 0:2]).then_inc(S[sub], 1)
                for sub in range(2):
                    dve.wait_ge(S[sub], at("indexf"))
                    for c, hot_c in enumerate((hot1, hot2)):
                        v.tensor_scalar(hot_c[:, bass.ds(2 * i + sub, 1), :].rearrange("p a e -> p (a e)"),
                                        ramp[:, 0:EXPERTS], idxf[:, sub, c:c + 1], None, ALU.is_equal)\
                            .then_inc(S[sub], 1)
                    v.tensor_copy(vals[:, bass.ds(2 * i + sub, 1), :].rearrange("p a e -> p (a e)"),
                                  top8[:, sub, 0:2]).then_inc(S[sub], 1)

            rounds(dve, NP_, router_tile)
            for sub in range(2):
                dve.wait_ge(s_rt_dve[sub], done(RT_DVE, "vals", NP_ - 1))

            v.tensor_tensor(dn[:, :], vals[:, :, 1], vals[:, :, 0], ALU.subtract).then_inc(s_exp, 1)
            for hot_c in (hot1, hot2):
                link(v.tensor_scalar(hot_c[:, NT - 1, :], hot_c[:, NT - 1, :], valid[:, 0:1], None, ALU.mult))
            v.tensor_tensor(chosen[:, :, :], hot1[:, :, :], hot2[:, :, :], ALU.add).then_inc(s_ch, 1)
            dve.wait_ge(s_exp, 2)
            link(v.tensor_scalar(dn[:, :], den[:, :], 1.0, None, ALU.add))
            link(v.reciprocal(gate[:, :, 0], dn[:, :]))
            v.tensor_tensor(gate[:, :, 1], gate[:, :, 0], den[:, :], ALU.mult).then_inc(s_gate, 1)
            dve.wait_ge(s_chp, 1)
            hh = NT // 2
            for q in range(2):
                view = bank[2 + q][:, 0:hh * EXPERTS].rearrange("p (t e) -> p t e", e=EXPERTS)
                link(v.tensor_copy(texp[:, q * hh:(q + 1) * hh, :], view))
            for e in range(EXPERTS):
                v.tensor_tensor_scan(slot[:, :, e], onesf[:, 0:NT], texp[:, :, e], 0.0, ALU.mult, ALU.add)\
                    .then_inc(s_m2, 1)
            dve.wait_ge(s_m2, EXPERTS)
            link(v.tensor_scalar(ebase[:, :], slot[:, NT - 1, :], float(P - 1), None, ALU.add))
            link(v.tensor_copy(etile_i[:, :], ebase[:, :]))
            link(v.tensor_scalar(etile_i[:, :], etile_i[:, :], 7, None, ALU.arith_shift_right))
            link(v.tensor_copy(etile[:, :], etile_i[:, :]))
            link(v.tensor_tensor_scan(eend[:, :], onesf[:, 0:EXPERTS], etile[:, :], 0.0, ALU.mult, ALU.add))
            v.sem_inc(s_ec, 1)
            link(v.tensor_tensor(ebase[:, :], eend[:, :], etile[:, :], ALU.subtract))
            link(v.tensor_scalar(ebase[:, :], ebase[:, :], float(P), None, ALU.mult))
            link(v.tensor_tensor(slot[:, :, :], slot[:, :, :], texp[:, :, :], ALU.subtract))
            link(v.tensor_tensor(slot[:, :, :], slot[:, :, :],
                                 ebase[:, :].unsqueeze(1).broadcast_to([P, NT, EXPERTS]), ALU.add))
            for q in range(2):
                view = bank[q][:, 0:hh * EXPERTS].rearrange("p (t e) -> p t e", e=EXPERTS)
                part = slot[:, q * hh:(q + 1) * hh, :]
                link(v.tensor_tensor(part, part, view, ALU.add))
            for c, hot_c in enumerate((hot1, hot2)):
                link(v.tensor_tensor(texp[:, :, :], slot[:, :, :], hot_c[:, :, :], ALU.mult))
                link(v.tensor_reduce(slots_f[:, :, c], texp[:, :, :], AX_X, ALU.add))
            link(v.tensor_copy(slots[:, :, :], slots_f[:, :, :]))
            dve.wait_ge(s_ecs, 1)
            link(v.tensor_copy(endcol[0:EXPERTS, :], bank[6][0:EXPERTS, 0:1]))
            v.tensor_scalar(past[0:EXPERTS, 0:ET], ramp[0:EXPERTS, 0:ET], endcol[0:EXPERTS, 0:1], None,
                            ALU.is_ge).then_inc(s_etp, 1)
            dve.wait_ge(s_ecs, 2)
            v.tensor_scalar(tile_expert[:, :], bank[7][0:1, 0:ET], float(EXPERTS - 1), None, ALU.min)\
                .then_inc(s_etab, 1)

            def slots_tile(i):
                for sub in range(2):
                    if not is_first(i):
                        held(dve, "dve", s_disp[sub], 32 * i)
                    v.tensor_copy(slot_st[:, sub, :],
                                  slots[:, bass.ds(2 * i + sub, 1), :].rearrange("p a e -> p (a e)"))\
                        .then_inc(s_st_dve[sub], 1)

            rounds(dve, NP_, slots_tile)

            dve.wait_ge(s_w, 16 * (2 * EXPERTS + 2))
            dve.wait_ge(s_etab, 1)

            def expert_tile(i):
                exp = [dve.value_load(tile_expert[0:1, bass.ds(2 * i + sub, 1)], min_val=0, max_val=EXPERTS - 1)
                       for sub in range(2)]
                for sub in range(2):
                    dve.wait_ge(s_ex_pe[sub], done(EX_PE, "up", i))
                    v.tensor_tensor(ex_u[:, sub, :], bank[4 * sub + 1][:, 0:HID],
                                    b1_sb[:, bass.ds(exp[sub], 1), :].rearrange("p a n -> p (a n)"), ALU.add)\
                        .then_inc(s_ex_dve[sub], 1)
                for sub in range(2):
                    dve.wait_ge(s_ex_pe[sub], done(EX_PE, "hT", i))
                    v.tensor_copy(ex_hT[:, sub, :], bank[4 * sub + 2][:, :]).then_inc(s_ex_dve[sub], 1)
                for sub in range(2):
                    if not is_first(i):
                        dve.wait_ge(s_exst[sub], 16 * i)
                    dve.wait_ge(s_ex_pe[sub], done(EX_PE, "down", i))
                    v.tensor_tensor(ex_y[:, sub, :], bank[4 * sub + 3][:, 0:D],
                                    b2_sb[:, bass.ds(exp[sub], 1), :].rearrange("p a n -> p (a n)"), ALU.add)\
                        .then_inc(s_ex_dve[sub], 1)

            rounds(dve, ET // 2, expert_tile)

            dve.wait_ge(s_gate, 1)

            def combine_tile(i):
                for sub in range(2):
                    if is_first(i):
                        dve.wait_ge(s_disp[sub], 32 * NP_)
                        v.tensor_copy(slot_st[:, sub, :], slots[:, sub, :]).then_inc(s_cidx[sub], 1)
                for sub in range(2):
                    t = 2 * i + sub
                    dve.wait_ge(s_cx[sub], 16 * (i + 1))
                    dve.wait_ge(s_cg[sub], 32 * (i + 1))
                    v.scalar_tensor_tensor(out=x1b[:, sub, :], in0=ya1[:, sub, :],
                                           scalar=gate[:, bass.ds(t, 1), 0], in1=x1b[:, sub, :],
                                           op0=ALU.mult, op1=ALU.add).then_inc(s_cdve[sub], 1)
                    dve.wait_ge(s_cdve[sub], 2 * i + 1)
                    if not is_first(i):
                        dve.wait_ge(s_out[sub], 16 * i)
                    v.scalar_tensor_tensor(out=zb[:, sub, :], in0=ya2[:, sub, :],
                                           scalar=gate[:, bass.ds(t, 1), 1], in1=x1b[:, sub, :],
                                           op0=ALU.mult, op1=ALU.add).then_inc(s_cdve[sub], 1)
                    if not is_last(i, NP_):
                        v.tensor_copy(slot_st[:, sub, :],
                                      slots[:, bass.ds(t + 2, 1), :].rearrange("p a e -> p (a e)"))\
                            .then_inc(s_cidx[sub], 1)

            rounds(dve, NP_, combine_tile)


_INS = ['x', 'src', 'dst', 'edge_weight', 'L0_gnn_weight', 'L0_gnn_b', 'L0_ffn_gamma', 'L0_ffn_beta',
        'L0_ffn_Wr', 'L0_ffn_br', 'L0_ffn_W1', 'L0_ffn_b1', 'L0_ffn_W2', 'L0_ffn_b2']


def kernel(**inputs):
    import numpy as _np
    import concourse.bacc as _bacc
    from concourse import mybir as _mybir
    from concourse.bass_utils import run_bass_kernel_spmd as _run

    nc = _bacc.Bacc("TRN2", target_bir_lowering=False, num_devices=1)
    arrays, args = {}, []
    for name in _INS:
        a = _np.ascontiguousarray(inputs[name])
        arrays[f"in_{name}_dram"] = a
        args.append(nc.dram_tensor(f"in_{name}_dram", a.shape, _mybir.dt.from_np(a.dtype), kind="ExternalInput").ap())
    args.append(nc.dram_tensor("out_0_dram", (NODES, D), _mybir.dt.float32, kind="ExternalOutput").ap())
    gnn_moe(nc, *args)
    r = _run(nc, [arrays], core_ids=[0])
    return r.results[0]["out_0_dram"]
```

```python
from contextlib import ExitStack

import concourse.bass as bass
from concourse import mybir

F32 = mybir.dt.float32
I32 = mybir.dt.int32
U32 = mybir.dt.uint32
BF16 = mybir.dt.bfloat16
F16 = mybir.dt.float16
ALU = mybir.AluOpType
ACT = mybir.ActivationFunctionType
AX_X = mybir.AxisListType.X

P = 128
NODES, D = 12500, 256
EDGES = 200000
EXPERTS, HID = 8, 512
EPS = 1e-5
NT = -(-NODES // P)
TAIL = NODES - (NT - 1) * P
KD, KH = D // P, HID // P
PER = 16
COLS = NT * PER
assert COLS * P >= EDGES
LAST = EDGES - (P - 1) * COLS
assert 0 < LAST <= COLS
BINS = NT + 1
GRP = 4
GRPS = PER // GRP
CHAINS = 2 * GRP
STEPS = -(-((EDGES + NT * (P - 1)) // P) // (2 * PER)) * 2
SLOTT = STEPS * PER
NSLOT = SLOTT * P
FAR = 1 << 20
BEYOND = float(1 << 25)
EROWS = 2 * P
NE = (2 * NODES + EXPERTS * (EROWS - 1)) // EROWS
NE += NE % 2
FILLS = 16
ZROWS = 4
assert NE * EROWS % (P * ZROWS) == 0
LANES = 7
TURNS = NT // LANES
assert TURNS * LANES == NT and TURNS % 2 == 0
HL = 2 * D
WSCALE = 64.0
HUGE = 3.0e38


def done(steps, name, i):
    return i * len(steps) + steps.index(name) + 1


def rounds(eng, n, body):
    body(0)
    with eng.Fori(1, n - 1) as i:
        body(i)
    body(n - 1)


def is_first(i):
    return isinstance(i, int) and i == 0


def is_last(i, n):
    return isinstance(i, int) and i == n - 1


LN_DVE = ("stats", "aggr", "rstd", "norm")
LN_ACT = ("std", "nT", "h")
LN_PE = ("nT", "h")
POS = ("int", "row", "col", "addr", "rec")
RT_DVE = ("stats1", "aggr1", "rstd1", "shift1", "stats2", "aggr2", "scaled", "rstd2", "xn")
RT_ACT = ("std1", "std2", "high")
EX_PE = ("up_a", "up_b", "down")
EX_ACT = ("gelu_a", "gelu_b")
EX_DVE = ("high_a", "low_a", "high_b", "low_b", "y")


def gnn_moe(nc, x, src, dst, edge_weight, gw, gb, gamma, beta, wr, br, w1, b1, w2, b2, out):
    h_rows = nc.dram_tensor("h_rows", (NT * P, D), F32).ap()
    edges_sorted = nc.dram_tensor("edges_sorted", (NSLOT, 4), I32).ap()
    x1_rows = nc.dram_tensor("x1_rows", (NT * P, D), F32).ap()
    xn_rows = nc.dram_tensor("xn_rows", (NT * P, HL), F16).ap()
    expert_in = nc.dram_tensor("expert_in", (NE * EROWS, HL), F16).ap()
    expert_out = nc.dram_tensor("expert_out", (NE * EROWS, D), F32).ap()

    with ExitStack() as ctx:
        def sb(name, shape, dt=F32):
            return ctx.enter_context(nc.sbuf_tensor(name, shape, dt))

        def sem(name):
            return ctx.enter_context(nc.semaphore(name))

        def sem2(name):
            return [sem(f"{name}{i}") for i in range(2)]

        acc = sb("acc", [P, NT, D])
        flat = acc[:, :, :].rearrange("p t d -> p (t d)")
        wsize = EXPERTS * KD * HID // 2
        w1h, w1l = (flat[:, k * wsize:(k + 1) * wsize].bitcast(F16)
                    .rearrange("p (e k n) -> p e k n", e=EXPERTS, k=KD) for k in range(2))
        w2h, w2l = (flat[:, k * wsize:(k + 1) * wsize].bitcast(F16)
                    .rearrange("p (e k n) -> p e k n", e=EXPERTS, k=KH) for k in range(2, 4))
        b2_sb = flat[:, 4 * wsize:4 * wsize + EXPERTS * D].rearrange("p (e n) -> p e n", e=EXPERTS)
        assert 4 * wsize + EXPERTS * D <= NT * D
        csize = 2 * LANES * D
        got1, got2, x1_in, summed = (flat[:, k * csize:(k + 1) * csize]
                                     .rearrange("p (b s n) -> p b s n", b=2, s=LANES) for k in range(4))

        recs = sb("recs", [P, COLS, 4], I32)
        recs_f = recs[:, :, :].bitcast(F32)
        bins16 = sb("bins16", [P, COLS], BF16)
        src_sb, dst_sb = (flat[:, k * COLS:(k + 1) * COLS].bitcast(I32) for k in range(2))
        ew_sb = flat[:, 2 * COLS:3 * COLS]
        ramp_i = flat[:, 3 * COLS:3 * COLS + SLOTT].bitcast(I32)
        late = recs_f.rearrange("p t w -> p (t w)")
        y_rt, xn_rt, xnT_rt = (late[:, k * LANES * D:(k + 1) * LANES * D].rearrange("p (s n) -> p s n", s=LANES)
                               for k in range(3))
        hot1, hot2, texp, slot, masked = (late[:, k * NT * EXPERTS:(k + 1) * NT * EXPERTS]
                                          .rearrange("p (t e) -> p t e", e=EXPERTS) for k in range(5))
        w_in = late[:, 0:4 * KD * HID].rearrange("p (b w n) -> p b w n", b=2, w=2)
        ex_xT = late[:, 0:4 * EROWS].bitcast(F16).rearrange("p (s n) -> p s n", s=2)
        ex_hh, ex_hl = (late[:, 4 * EROWS * (1 + k):4 * EROWS * (2 + k)].bitcast(F16)
                        .rearrange("p (s n) -> p s n", s=2) for k in range(2))
        fill = sb("fill", [P, SLOTT // FILLS, 4], I32)
        fill_f = fill[:, :, :].bitcast(F32)
        ramp = sb("ramp", [P, SLOTT])
        past = sb("past", [P, SLOTT], BF16)
        zeros = sb("zeros", [P, ZROWS * D])
        tri = sb("tri", [P, P], BF16)
        rest = sb("rest", [P, P], BF16)
        ones = sb("ones", [P, P], BF16)
        onesf = sb("onesf", [P, P])
        ident = sb("ident", [P, P])
        ident16 = sb("ident16", [P, P], F16)
        valid = sb("valid", [P, 1])
        eps = sb("eps", [P, 1])
        gw_sb = sb("gw_sb", [P, KD, D])
        gb_sb = sb("gb_sb", [P, D])
        gamma_sb = sb("gamma_sb", [P, D])
        beta_sb = sb("beta_sb", [P, D])
        wr_sb = sb("wr_sb", [P, KD, EXPERTS])
        br_sb = sb("br_sb", [P, EXPERTS])
        hot = sb("hot", [P, 2, BINS, PER], BF16)
        numbers = sb("numbers", [P, BINS, PER], BF16)
        prod = sb("prod", [P, 2, BINS, GRP])
        rows = sb("rows", [P, PER, D])
        rows_flat = rows[:, :, :].rearrange("p k d -> p (k d)")
        pairs_out = rows_flat[:, 0:LANES * D].bitcast(F16).rearrange("p (s n) -> p s n", s=LANES)
        pairs_in = rows_flat[:, 0:2 * LANES * D].bitcast(F16).rearrange("p (b s n) -> p b s n", b=2, s=LANES)
        ex_h = rows_flat[:, 0:8 * EROWS].rearrange("p (s n) -> p s n", s=2)
        ex_y = rows_flat[:, 8 * EROWS:12 * EROWS].rearrange("p (s h n) -> p s h n", s=2, h=2)
        ex_x = rows_flat[:, 12 * EROWS:16 * EROWS].bitcast(F16).rearrange("p (s h n) -> p s h n", s=2, h=2)
        totals, base = (rows_flat[:, k * CHAINS * BINS:(k + 1) * CHAINS * BINS]
                        .rearrange("p (c b) -> p c b", c=CHAINS) for k in range(2))
        binsum = sb("binsum", [P, BINS])
        bintile_i = sb("bintile_i", [P, BINS], I32)
        bintile = sb("bintile", [P, BINS])
        binend = sb("binend", [P, BINS])
        endcol = sb("endcol", [P, 1])
        tile_bin = sb("tile_bin", [1, SLOTT], I32)
        pos = sb("pos", [P, 2, PER])
        pos_i = sb("pos_i", [P, 2, PER], I32)
        pos_row = sb("pos_row", [P, 2, PER], I32)
        pos_col = sb("pos_col", [P, 2, PER], I32)
        addr = sb("addr", [P, 2, PER], I32)
        rec_out = sb("rec_out", [P, 2, PER, 4], I32)
        xin = sb("xin", [P, 2, D])
        stats = sb("stats", [P, 2, 6])
        mv = sb("mv", [P, 2, 2])
        std = sb("std", [P, 2, 1])
        rstd = sb("rstd", [P, 2, 1])
        normed = sb("normed", [P, 2, D])
        normedT = sb("normedT", [P, 2, D])
        h_out = sb("h_out", [P, 2, D])
        rec_in = sb("rec_in", [P, 2, PER, 4], I32)
        rec_in_f = rec_in[:, :, :, :].bitcast(F32)
        pick = sb("pick", [P, 4, P])
        stats_rt = sb("stats_rt", [P, LANES, 6])
        mv_rt = sb("mv_rt", [P, LANES, 2])
        std_rt = sb("std_rt", [P, LANES])
        shift_rt = sb("shift_rt", [P, LANES])
        rstd_rt = sb("rstd_rt", [P, LANES])
        logits = sb("logits", [P, NT, EXPERTS])
        em8 = sb("em8", [P, EXPERTS])
        picked = sb("picked", [P, NT])
        b1_rows = sb("b1_rows", [EXPERTS * KH, P])
        b1T = sb("b1T", [P, EXPERTS * KH])
        vals = sb("vals", [P, NT, 2])
        gate = sb("gate", [P, NT, 2])
        chosen = sb("chosen", [P, NT, EXPERTS], BF16)
        slots_f = sb("slots_f", [P, NT, 2])
        slots = sb("slots", [P, NT, 2], I32)
        eend = sb("eend", [P, EXPERTS])
        etile = sb("etile", [P, EXPERTS])
        etile_i = sb("etile_i", [P, EXPERTS], I32)
        ebase = sb("ebase", [P, EXPERTS])
        tile_expert = sb("tile_expert", [1, NE], I32)
        dn = sb("dn", [P, NT])
        den = sb("den", [P, NT])
        slot_st = sb("slot_st", [P, 2, LANES, 2], I32)

        bank = [ctx.enter_context(nc.psum_tensor(f"bank{i}", [P, 512], F32)) for i in range(8)]
        NG = GRP * BINS
        assert NG <= 512

        def counts(b):
            return bank[b][:, 0:NG].rearrange("p (b c) -> p b c", c=GRP)

        def hot_of(sub, gidx):
            return hot[:, sub, :, GRP * gidx:GRP * gidx + GRP]

        s_src, s_edge, s_par = sem("s_src"), sem("s_edge"), sem("s_par")
        s_const, s_made, s_recs = sem("s_const"), sem("s_made"), sem("s_recs")
        s_fill, s_zero, s_zeroed = sem("s_fill"), sem("s_zero"), sem("s_zeroed")
        s_hot, s_hist = sem("s_hot"), sem("s_hist")
        s_mid, s_base, s_based, s_colT, s_ends, s_tbl = (sem(n) for n in (
            "s_mid", "s_base", "s_based", "s_colT", "s_ends", "s_tbl"))
        s_rank, s_read, s_count, s_red, s_pos = (sem(n) for n in (
            "s_rank", "s_read", "s_count", "s_red", "s_pos"))
        s_scat = sem2("s_scat")
        s_xin, s_ln_dve, s_ln_act, s_ln_pe, s_hst = (sem2(n) for n in (
            "s_xin", "s_ln_dve", "s_ln_act", "s_ln_pe", "s_hst"))
        s_recin = sem2("s_recin")
        s_row = [sem(f"s_row{k}") for k in range(PER)]
        s_pick, s_sum, s_acc = sem("s_pick"), sem("s_sum"), sem("s_acc")
        s_rt_dve, s_rt_act, s_rtT_pe, s_rtT_act, s_lg_pe, s_lg_act, s_x1st, s_xnst = (sem(n) for n in (
            "s_rt_dve", "s_rt_act", "s_rtT_pe", "s_rtT_act", "s_lg_pe", "s_lg_act", "s_x1st", "s_xnst"))
        s_y, s_low = sem("s_y"), sem("s_low")
        s_b1, s_b1T, s_b1c, s_b2 = sem("s_b1"), sem("s_b1T"), sem("s_b1c"), sem("s_b2")
        s_ch, s_chp, s_m2, s_exp, s_ec, s_ecs, s_past, s_etp = (sem(n) for n in (
            "s_ch", "s_chp", "s_m2", "s_exp", "s_ec", "s_ecs", "s_past", "s_etp"))
        s_slots, s_etab = sem("s_slots"), sem("s_etab")
        s_pin, s_st_dve, s_disp = sem2("s_pin"), sem2("s_st_dve"), sem2("s_disp")
        s_win, s_whigh, s_wlow = sem2("s_win"), sem("s_whigh"), sem("s_wlow")
        s_exin, s_ex_pe, s_ex_act, s_ex_dve, s_exst = (
            sem2("s_exin"), sem2("s_ex_pe"), sem2("s_ex_act"), sem2("s_ex_dve"), sem2("s_exst"))
        s_exT_pe, s_exT_act = sem2("s_exT_pe"), sem2("s_exT_act")
        s_cx, s_cidx, s_cg, s_cdve, s_out = (sem2(n) for n in (
            "s_cx", "s_cidx", "s_cg", "s_cdve", "s_out"))
        s_numbers = sem("s_numbers")
        s_gate, s_cleared = sem("s_gate"), sem("s_cleared")
        s_held = {n: sem(f"s_held_{n}") for n in ("pool", "act", "dve")}

        def held(eng, which, s, value):
            eng.wait_ge(s, value)
            eng.sem_inc(s_held[which], 1)

        def loads(eng, ap, top):
            return nc.values_load_multi_w_load_instructions(
                ap, engines=(eng.engine,), min_val=0, max_val=top, skip_runtime_bounds_check_because="a table of the program's own")[1]

        x_rows = x
        NP_ = NT // 2
        assert NT % 2 == 0 and STEPS % 2 == 0

        block = ctx.enter_context(nc.Block())

        @block.sync
        def _(sp):
            def spread(ap, dst_sb, s):
                full = (P - 1) * COLS
                sp.dma_start(dst_sb[0:P - 1, :], ap[0:full].rearrange("(p t) -> p t", t=COLS)).then_inc(s, 16)
                sp.dma_start(dst_sb[P - 1:P, 0:LAST], ap[full:EDGES].rearrange("(p t) -> p t", p=1)).then_inc(s, 16)

            sp.wait_ge(s_made, 3)
            spread(src, src_sb, s_src)
            spread(dst, dst_sb, s_edge)
            spread(edge_weight, ew_sb, s_edge)
            sp.dma_start(gw_sb[:, :, :], gw.rearrange("(k p) n -> p k n", p=P)).then_inc(s_par, 16)
            sp.dma_start(wr_sb[:, :, :], wr.rearrange("(k p) n -> p k n", p=P)).then_inc(s_par, 16)
            sp.dma_start(b1_rows[:, :], b1.rearrange("e (c p) -> (e c) p", p=P)).then_inc(s_b1, 16)
            for ap, t in ((gb, gb_sb), (gamma, gamma_sb), (beta, beta_sb), (br, br_sb)):
                sp.dma_start(t[:, :], ap.partition_broadcast(P)).then_inc(s_par, 16)
            sp.wait_ge(s_zero, 2)
            part = SLOTT // FILLS
            grid = edges_sorted.rearrange("(p t) w -> p t w", p=P)
            for k in range(FILLS):
                sp.dma_start(grid[:, k * part:(k + 1) * part, :], fill[:, :, :]).then_inc(s_fill, 16)
            zgrid = expert_in.rearrange("(p t) d -> p (t d)", p=P)
            zn = ZROWS * HL
            for k in range(NE * EROWS // (P * ZROWS)):
                sp.dma_start(zgrid[:, k * zn:(k + 1) * zn],
                             zeros[:, :].bitcast(F16)).then_inc(s_zeroed, 16)

            def node_tile(i):
                for sub in range(2):
                    t = 2 * i + sub
                    n = TAIL if is_last(i, NP_) and sub else P
                    if not is_first(i):
                        sp.wait_ge(s_ln_dve[sub], done(LN_DVE, "norm", i - 1))
                    sp.dma_start(xin[0:n, sub, :], x_rows[bass.ds(t * P, n), :]).then_inc(s_xin[sub], 16)
                for sub in range(2):
                    t = 2 * i + sub
                    sp.wait_ge(s_ln_act[sub], done(LN_ACT, "h", i))
                    sp.dma_start(h_rows[bass.ds(t * P, P), :], h_out[:, sub, :]).then_inc(s_hst[sub], 16)

            rounds(sp, NP_, node_tile)

            for sub in range(2):
                sp.wait_ge(s_scat[sub], 16 * PER * NP_)

            def sorted_step(i):
                for sub in range(2):
                    step = 2 * i + sub
                    if not is_first(i):
                        sp.wait_ge(s_sum, PER * (step - 1))
                    sp.dma_start(rec_in[:, sub, :, :],
                                 grid[:, bass.ds(step * PER, PER), :]).then_inc(s_recin[sub], 16)

            rounds(sp, STEPS // 2, sorted_step)

            x1_grid = x1_rows.rearrange("(t p) d -> p t d", p=P)
            xn_grid = xn_rows.rearrange("(t p) d -> p t d", p=P)
            sp.wait_ge(s_acc, SLOTT)
            for k in range(LANES):
                sp.dma_start(x1_grid[:, k * TURNS:(k + 1) * TURNS, :],
                             acc[:, k * TURNS:(k + 1) * TURNS, :]).then_inc(s_x1st, 16)

            def router_turn(i):
                sp.wait_ge(s_low, i + 1)
                sp.dma_start(xn_grid[:, bass.ds(LANES * i, LANES), :], pairs_out).then_inc(s_xnst, 16)

            rounds(sp, TURNS, router_turn)

            sp.wait_ge(s_xnst, 16 * TURNS)

            def dispatch_turns(i):
                for b in range(2):
                    if not is_first(i):
                        sp.wait_ge(s_disp[b], 32 * LANES * i)
                    sp.dma_start(pairs_in[:, b], xn_grid[:, bass.ds(LANES * (2 * i + b), LANES), :])\
                        .then_inc(s_pin[b], 16)

            rounds(sp, TURNS // 2, dispatch_turns)

            for b in range(2):
                sp.wait_ge(s_disp[b], 32 * LANES * (TURNS // 2))
            sp.wait_ge(s_wlow, 2 * EXPERTS)
            in_grid = expert_in.rearrange("(t p) d -> p t d", p=P)
            out_grid = expert_out.rearrange("(t p) d -> p t d", p=P)

            def load_rows(i, sub):
                sp.dma_start(ex_x[:, sub], in_grid[:, bass.ds(2 * (2 * i + sub), 2), :]).then_inc(s_exin[sub], 16)

            for sub in range(2):
                load_rows(0, sub)

            def expert_step(i):
                if not is_last(i, NE // 2):
                    for sub in range(2):
                        sp.wait_ge(s_exT_pe[sub], i + 1)
                        load_rows(i + 1, sub)
                for sub in range(2):
                    sp.wait_ge(s_ex_dve[sub], done(EX_DVE, "y", i))
                    sp.dma_start(out_grid[:, bass.ds(2 * (2 * i + sub), 2), :], ex_y[:, sub])\
                        .then_inc(s_exst[sub], 16)

            rounds(sp, NE // 2, expert_step)

            for sub in range(2):
                sp.wait_ge(s_exst[sub], 16 * (NE // 2))
            out_full = out[0:(NT - 1) * P, :].rearrange("(t p) d -> p t d", p=P)

            def combine_turns(i):
                for b in range(2):
                    if not is_first(i):
                        sp.wait_ge(s_cdve[b], 2 * LANES * i)
                    sp.dma_start(x1_in[:, b], x1_grid[:, bass.ds(LANES * (2 * i + b), LANES), :])\
                        .then_inc(s_cx[b], 16)
                for b in range(2):
                    n = LANES - 1 if is_last(i, TURNS // 2) and b else LANES
                    sp.wait_ge(s_cdve[b], 2 * LANES * (i + 1))
                    sp.dma_start(out_full[:, bass.ds(LANES * (2 * i + b), n), :], summed[:, b, 0:n, :])\
                        .then_inc(s_out[b], 16)

            rounds(sp, TURNS // 2, combine_turns)
            sp.dma_start(out[(NT - 1) * P:NODES, :], summed[0:TAIL, 1, LANES - 1, :]).then_inc(s_out[1], 16)
            sp.wait_ge(s_out[0], 16 * (TURNS // 2))
            sp.wait_ge(s_out[1], 16 * (TURNS // 2) + 16)

        @block.gpsimd
        def _(pool):
            g = nc.gpsimd
            g.iota(ramp_i, [[1, SLOTT]], base=0, channel_multiplier=0).then_inc(s_const, 1)
            g.iota(numbers[:, :, :], [[1, BINS], [0, PER]], base=0, channel_multiplier=0,
                   allow_small_or_imprecise_dtypes=True).then_inc(s_numbers, 1)
            g.memset(tri[:, :], 1.0).then_inc(s_const, 1)
            g.memset(rest[:, :], 1.0).then_inc(s_const, 1)
            g.memset(ident[:, :], 0.0).then_inc(s_const, 1)
            g.memset(valid[:, :], 1.0).then_inc(s_const, 1)
            pool.wait_ge(s_const, 5)
            g.affine_select(out=tri[:, :], in_=tri[:, :], compare_op=ALU.is_gt, fill=0.0, base=0,
                            pattern=[[1, P]], channel_multiplier=-1).then_inc(s_const, 1)
            g.affine_select(out=rest[:, :], in_=rest[:, :], compare_op=ALU.is_ge, fill=0.0, base=0,
                            pattern=[[-1, P]], channel_multiplier=1).then_inc(s_const, 1)
            g.affine_select(out=ident[:, :], in_=ident[:, :], compare_op=ALU.not_equal, fill=1.0, base=0,
                            pattern=[[-1, P]], channel_multiplier=1).then_inc(s_const, 1)
            g.affine_select(out=valid[:, :], in_=valid[:, :], compare_op=ALU.is_ge, fill=0.0, base=TAIL - 1,
                            pattern=[[0, 1]], channel_multiplier=-1).then_inc(s_const, 1)
            g.memset(zeros[:, :], 0.0).then_inc(s_zero, 1)

            pool.wait_ge(s_fill, 16 * FILLS)

            def scatter_step(i):
                for sub in range(2):
                    held(pool, "pool", s_pos, done(POS, "rec", 2 * i + sub))
                    for k in range(PER):
                        pool.indirect_dma_start(
                            out=edges_sorted[:, :],
                            out_offset=bass.IndirectOffsetOnAxis(ap=addr[:, sub, k:k + 1], axis=0),
                            in_=rec_out[:, sub, k, :], in_offset=None,
                            bounds_check=NSLOT - 1, oob_is_err=False).then_inc(s_scat[sub], 16)

            rounds(pool, NP_, scatter_step)

            pool.wait_ge(s_cleared, 2)
            for sub in range(2):
                pool.wait_ge(s_hst[sub], 16 * NP_)

            def gather_step(i):
                for sub in range(2):
                    step = 2 * i + sub
                    held(pool, "pool", s_recin[sub], 16 * (i + 1))
                    for k in range(PER):
                        if k % 4 == 0 and not (is_first(i) and sub == 0):
                            held(pool, "pool", s_sum, PER * step - PER + k + 4)
                        pool.indirect_dma_start(
                            out=rows[:, k, :], out_offset=None, in_=h_rows[:, :],
                            in_offset=bass.IndirectOffsetOnAxis(ap=rec_in[:, sub, k, 0:1], axis=0),
                            bounds_check=NODES - 1, oob_is_err=False).then_inc(s_row[k], 16)

            rounds(pool, STEPS // 2, gather_step)

            zero_stores = NE * EROWS // (P * ZROWS)
            pool.wait_ge(s_zeroed, 16 * zero_stores)

            def dispatch_turns(i):
                for b in range(2):
                    held(pool, "pool", s_pin[b], 16 * (i + 1))
                    held(pool, "pool", s_st_dve[b], i + 1)
                    for k in range(LANES):
                        n = TAIL if is_last(i, TURNS // 2) and b and k == LANES - 1 else P
                        for c in range(2):
                            pool.indirect_dma_start(
                                out=expert_in[:, :],
                                out_offset=bass.IndirectOffsetOnAxis(ap=slot_st[0:n, b, k, c:c + 1], axis=0),
                                in_=pairs_in[0:n, b, k, :], in_offset=None,
                                bounds_check=NE * EROWS - 1, oob_is_err=False).then_inc(s_disp[b], 16)

            rounds(pool, TURNS // 2, dispatch_turns)

            for sub in range(2):
                pool.wait_ge(s_exst[sub], 16 * (NE // 2))

            def fetch_turns(i):
                for b in range(2):
                    held(pool, "pool", s_cidx[b], i + 1)
                    for k in range(LANES):
                        n = TAIL if is_last(i, TURNS // 2) and b and k == LANES - 1 else P
                        for c, got in enumerate((got1, got2)):
                            pool.indirect_dma_start(
                                out=got[0:n, b, k, :], out_offset=None, in_=expert_out[:, :],
                                in_offset=bass.IndirectOffsetOnAxis(ap=slot_st[0:n, b, k, c:c + 1], axis=0),
                                bounds_check=NE * EROWS - 1, oob_is_err=False).then_inc(s_cg[b], 16)

            rounds(pool, TURNS // 2, fetch_turns)

        @block.tensor
        def _(pe):
            mm = nc.tensor.matmul
            pe.wait_ge(s_made, 7)
            pe.wait_ge(s_const, 9)

            def hist_step(i):
                for sub in range(2):
                    pe.wait_ge(s_hot, 2 * i + sub + 1)
                    for gidx in range(GRPS):
                        last = mm(counts(gidx % 2), ones[:, :], hot_of(sub, gidx),
                                  start=is_first(i) and sub == 0 and gidx < 2,
                                  stop=is_last(i, NP_) and sub == 1 and gidx >= GRPS - 2, skip_group_check=True)
                    last.then_inc(s_hist, 1)

            rounds(pe, NP_, hist_step)

            pe.wait_ge(s_ends, 1)
            mm(bank[2][0:NT, 0:1], binend[0:1, 0:NT], onesf[0:1, 0:1], start=True, stop=True).then_inc(s_colT, 1)
            pe.wait_ge(s_base, 1)
            for b in range(2):
                mm(counts(b), onesf[0:1, :], base[0:1, GRP * b:GRP * b + GRP, :].rearrange("p c b -> p b c"), start=True, stop=False,
                   skip_group_check=True).then_inc(s_based, 1)
            pe.wait_ge(s_past, 1)
            quarter = SLOTT // 4
            for q in range(4):
                mm(bank[3 + q][0:1, 0:quarter], ones[0:NT, 0:1], past[0:NT, q * quarter:(q + 1) * quarter],
                   start=True, stop=True).then_inc(s_tbl, 1)
            pe.wait_ge(s_tbl, 8)

            def rank(t, sub, gidx):
                if gidx == 0:
                    pe.wait_ge(s_hot, t + (NT + 1))
                mm(counts(gidx % 2), tri[:, :], hot_of(sub, gidx), start=False, stop=False,
                   skip_group_check=True).then_inc(s_rank, 1)

            def count(t, sub, gidx):
                pe.wait_ge(s_read, GRPS * t + gidx + 1)
                mm(counts(gidx % 2), rest[:, :], hot_of(sub, gidx), start=False, stop=False,
                   skip_group_check=True).then_inc(s_count, 1)

            def ln_T(i, sub):
                pe.wait_ge(s_ln_dve[sub], done(LN_DVE, "norm", i))
                for k in range(KD):
                    last = nc.tensor.transpose(bank[2 + sub][:, k * P:(k + 1) * P],
                                               normed[:, sub, k * P:(k + 1) * P], ident[:, :])
                last.then_inc(s_ln_pe[sub], 1)

            def ln_h(i, sub):
                pe.wait_ge(s_ln_act[sub], done(LN_ACT, "nT", i))
                for k in range(KD):
                    last = mm(bank[4 + sub][:, 0:D], normedT[:, sub, k * P:(k + 1) * P], gw_sb[:, k, :],
                              start=(k == 0), stop=(k == KD - 1))
                last.then_inc(s_ln_pe[sub], 1)

            pe.wait_ge(s_b1, 16)
            nc.tensor.transpose(bank[7][:, 0:EXPERTS * KH], b1_rows[:, :], ident[0:EXPERTS * KH, 0:EXPERTS * KH])\
                .then_inc(s_b1T, 1)
            pe.wait_ge(s_par, 16 * 6)

            def sort_step(i):
                for sub in range(2):
                    t = 2 * i + sub
                    rank(t, sub, 0)
                    rank(t, sub, 1)
                    count(t, sub, 0)
                    rank(t, sub, 2)
                    count(t, sub, 1)
                    rank(t, sub, 3)
                    count(t, sub, 2)
                    count(t, sub, 3)
                    if sub == 0:
                        ln_T(i, 0)
                ln_h(i, 0)
                ln_T(i, 1)
                ln_h(i, 1)

            rounds(pe, NP_, sort_step)

            for sub in range(2):
                pe.wait_ge(s_ln_act[sub], done(LN_ACT, "h", NP_ - 1))

            def sum_step(i):
                for sub in range(2):
                    for k in range(PER):
                        n = PER * (2 * i + sub) + k
                        pe.wait_ge(s_pick, n + 1)
                        pe.wait_ge(s_row[k], 16 * (2 * i + sub + 1))
                        if not (is_first(i) and sub == 0 and k < 4):
                            pe.wait_ge(s_acc, n - 3)
                        mm(bank[k % 4][:, 0:D], pick[:, k % 4, :], rows[:, k, :],
                           start=True, stop=True).then_inc(s_sum, 1)

            rounds(pe, STEPS // 2, sum_step)

            def router_turn(i):
                pe.wait_ge(s_rt_dve, done(RT_DVE, "xn", i))
                for k in range(LANES):
                    if not is_first(i):
                        pe.wait_ge(s_rtT_act, LANES * i - LANES + k + 1)
                    for c in range(KD):
                        last = nc.tensor.transpose(bank[k][:, c * P:(c + 1) * P],
                                                   xn_rt[:, k, c * P:(c + 1) * P], ident[:, :])
                    last.then_inc(s_rtT_pe, 1)
                for k in range(LANES):
                    pe.wait_ge(s_rtT_act, LANES * i + k + 1)
                    if k:
                        pe.wait_ge(s_lg_act, LANES * i + k)
                    elif not is_first(i):
                        pe.wait_ge(s_lg_act, LANES * i)
                    for c in range(KD):
                        last = mm(bank[7][:, 0:EXPERTS], xnT_rt[:, k, c * P:(c + 1) * P], wr_sb[:, c, :],
                                  start=(c == 0), stop=(c == KD - 1))
                    last.then_inc(s_lg_pe, 1)

            pe.wait_ge(s_acc, SLOTT)
            rounds(pe, TURNS, router_turn)

            half = NT // 2 * EXPERTS
            ch = chosen[:, :, :].rearrange("p t e -> p (t e)")
            pe.wait_ge(s_ch, 1)
            for q in range(2):
                mm(bank[q][:, 0:half], tri[:, :], ch[:, q * half:(q + 1) * half], start=True, stop=True)
            for q in range(2):
                last = mm(bank[2 + q][:, 0:half], ones[:, :], ch[:, q * half:(q + 1) * half], start=True, stop=True)
            last.then_inc(s_chp, 1)
            pe.wait_ge(s_ec, 1)
            mm(bank[6][0:EXPERTS, 0:1], eend[0:1, 0:EXPERTS], onesf[0:1, 0:1], start=True, stop=True).then_inc(s_ecs, 1)
            pe.wait_ge(s_etp, 1)
            mm(bank[7][0:1, 0:NE], ones[0:EXPERTS, 0:1], past[0:EXPERTS, 0:NE], start=True, stop=True).then_inc(s_ecs, 1)

            pe.wait_ge(s_wlow, 2 * EXPERTS)
            pe.wait_ge(s_etab, 1)

            def pairs_mm(dst_ap, left, right, first, last_one):
                for n, (a, b) in enumerate(((0, 0), (0, 1), (1, 0))):
                    ins = mm(dst_ap, left[a], right[b], start=first and n == 0, stop=last_one and n == 2,
                             skip_group_check=True)
                return ins

            def turn_rows(i):
                for sub in range(2):
                    bT = bank[4 * sub][:, :].bitcast(F16).rearrange("p (q h n) -> p q h n", q=4, h=2)
                    pe.wait_ge(s_exin[sub], 16 * (i + 1))
                    for h in range(2):
                        for q in range(4):
                            last = nc.tensor.transpose(bT[:, q, h, :], ex_x[:, sub, h, q * P:(q + 1) * P],
                                                       ident16[:, :])
                    last.then_inc(s_exT_pe[sub], 1)

            turn_rows(0)

            def expert_step(i):
                exp = loads(pe, tile_expert[0:1, bass.ds(2 * i, 2)], EXPERTS - 1)
                for sub in range(2):
                    xT = ex_xT[:, sub, :].rearrange("p (w k n) -> p w k n", w=2, k=KD)
                    pe.wait_ge(s_exT_act[sub], i + 1)
                    for c in range(KH):
                        for k in range(KD):
                            w = [t[:, bass.ds(exp[sub], 1), k, c * P:(c + 1) * P].rearrange("p a n -> p (a n)")
                                 for t in (w1h, w1l)]
                            last = pairs_mm(bank[4 * sub + 1 + c // 2][:, c % 2 * EROWS:(c % 2 + 1) * EROWS],
                                            w, [xT[:, 0, k, :], xT[:, 1, k, :]], k == 0, k == KD - 1)
                        if c % 2:
                            last.then_inc(s_ex_pe[sub], 1)
                if not is_last(i, NE // 2):
                    turn_rows(i + 1)
                for sub in range(2):
                    pe.wait_ge(s_ex_dve[sub], done(EX_DVE, "low_b", i))
                    for h in range(2):
                        for c in range(KH):
                            at = c * EROWS + h * P
                            w = [t[:, bass.ds(exp[sub], 1), c, :].rearrange("p a n -> p (a n)")
                                 for t in (w2h, w2l)]
                            last = pairs_mm(bank[4 * sub + 3][:, h * D:(h + 1) * D],
                                            [ex_hh[:, sub, at:at + P], ex_hl[:, sub, at:at + P]], w,
                                            c == 0, c == KH - 1)
                    last.then_inc(s_ex_pe[sub], 1)

            rounds(pe, NE // 2, expert_step)

        @block.scalar
        def _(act):
            a = nc.scalar
            act.wait_ge(s_made, 7)

            def std_of(sub, s, wait_sem, value):
                act.wait_ge(wait_sem, value)
                a.activation(std[:, sub, :], mv[:, sub, 1:2], ACT.Sqrt, bias=eps[:, 0:1]).then_inc(s, 1)

            act.wait_ge(s_b1T, 1)
            a.copy(b1T[:, :], bank[7][:, 0:EXPERTS * KH]).then_inc(s_b1c, 1)

            def ln_tile(i):
                def take_T(sub):
                    act.wait_ge(s_ln_pe[sub], done(LN_PE, "nT", i))
                    a.copy(normedT[:, sub, :], bank[2 + sub][:, 0:D]).then_inc(s_ln_act[sub], 1)

                def take_h(sub):
                    if not is_first(i):
                        act.wait_ge(s_hst[sub], 16 * i)
                    act.wait_ge(s_ln_pe[sub], done(LN_PE, "h", i))
                    a.copy(h_out[:, sub, :], bank[4 + sub][:, 0:D]).then_inc(s_ln_act[sub], 1)

                std_of(0, s_ln_act[0], s_ln_dve[0], done(LN_DVE, "aggr", i))
                take_T(0)
                std_of(1, s_ln_act[1], s_ln_dve[1], done(LN_DVE, "aggr", i))
                take_h(0)
                take_T(1)
                take_h(1)

            rounds(act, NP_, ln_tile)

            def router_turn(i):
                def std_rt_of(name):
                    act.wait_ge(s_rt_dve, done(RT_DVE, name, i))
                    a.activation(std_rt[:, :], mv_rt[:, :, 1], ACT.Sqrt, bias=eps[:, 0:1]).then_inc(s_rt_act, 1)

                std_rt_of("aggr1")
                held(act, "act", s_rt_dve, done(RT_DVE, "shift1", i))
                for k in range(LANES):
                    a.activation(y_rt[:, k, :], acc[:, bass.ds(LANES * i + k, 1), :].rearrange("p a d -> p (a d)"),
                                 ACT.Identity, bias=shift_rt[:, k:k + 1], scale=rstd_rt[:, k:k + 1]).then_inc(s_y, 1)
                std_rt_of("aggr2")
                if not is_first(i):
                    act.wait_ge(s_xnst, 16 * i)
                act.wait_ge(s_rt_dve, done(RT_DVE, "xn", i))
                a.copy(pairs_out[:, :, 0:D], xn_rt).then_inc(s_rt_act, 1)
                for k in range(LANES):
                    act.wait_ge(s_rtT_pe, LANES * i + k + 1)
                    a.copy(xnT_rt[:, k, :], bank[k][:, 0:D]).then_inc(s_rtT_act, 1)
                for k in range(LANES):
                    held(act, "act", s_lg_pe, LANES * i + k + 1)
                    a.copy(logits[:, bass.ds(LANES * i + k, 1), :].rearrange("p a e -> p (a e)"),
                           bank[7][:, 0:EXPERTS]).then_inc(s_lg_act, 1)

            rounds(act, TURNS, router_turn)

            act.wait_ge(s_exp, 1)
            a.activation(den[:, :], dn[:, :], ACT.Exp).then_inc(s_exp, 1)

            act.wait_ge(s_x1st, 16 * LANES)
            act.wait_ge(s_slots, 1)
            act.dma_start(b2_sb, b2.partition_broadcast(P)).then_inc(s_b2, 16)

            def load_weights(e):
                act.dma_start(w_in[:, e % 2, 0, :].rearrange("p (k n) -> p k n", k=KD),
                              w1[e].rearrange("(k p) n -> p k n", p=P)).then_inc(s_win[e % 2], 16)
                act.dma_start(w_in[:, e % 2, 1, :].rearrange("p (k n) -> p k n", k=KH),
                              w2[e].rearrange("(k p) n -> p k n", p=P)).then_inc(s_win[e % 2], 16)

            load_weights(0)
            load_weights(1)
            for e in range(EXPERTS):
                act.wait_ge(s_win[e % 2], 32 * (e // 2 + 1))
                for n, t in enumerate((w1h, w2h)):
                    a.activation(t[:, e].rearrange("p k n -> p (k n)"), w_in[:, e % 2, n, :], ACT.Copy,
                                 scale=WSCALE).then_inc(s_whigh, 1)
                if e + 2 < EXPERTS:
                    act.wait_ge(s_wlow, 2 * e + 2)
                    load_weights(e + 2)

            act.wait_ge(s_etab, 1)
            act.wait_ge(s_wlow, 2 * EXPERTS)
            act.wait_ge(s_b1c, 1)

            def take_xT(i):
                for sub in range(2):
                    act.wait_ge(s_exT_pe[sub], i + 1)
                    a.copy(ex_xT[:, sub, :], bank[4 * sub][:, :].bitcast(F16)).then_inc(s_exT_act[sub], 1)

            take_xT(0)

            def expert_step(i):
                exp = loads(act, tile_expert[0:1, bass.ds(2 * i, 2)], EXPERTS - 1)
                for sub in range(2):
                    for half in range(2):
                        held(act, "act", s_ex_pe[sub], done(EX_PE, ("up_a", "up_b")[half], i))
                        for c in range(2 * half, 2 * half + 2):
                            last = a.activation(ex_h[:, sub, c * EROWS:(c + 1) * EROWS],
                                                bank[4 * sub + 1 + half][:, c % 2 * EROWS:(c % 2 + 1) * EROWS],
                                                ACT.Gelu, bias=b1T[:, bass.ds(exp[sub] * KH + c, 1)],
                                                scale=1.0 / WSCALE)
                        last.then_inc(s_ex_act[sub], 1)
                if not is_last(i, NE // 2):
                    take_xT(i + 1)

            rounds(act, NE // 2, expert_step)

        @block.vector
        def _(dve):
            v = nc.vector
            link_count = [0]

            def link(ins, s=s_mid):
                link_count[0] += 1
                ins.then_inc(s, 1)
                dve.wait_ge(s, link_count[0])

            v.memset(src_sb[:, :], NT * P).then_inc(s_made, 1)
            v.memset(dst_sb[:, :], 0).then_inc(s_made, 1)
            v.memset(ew_sb[:, :], 0.0).then_inc(s_made, 1)
            v.memset(ones[:, :], 1.0).then_inc(s_made, 1)
            v.memset(onesf[:, :], 1.0).then_inc(s_made, 1)
            v.memset(eps[:, :], EPS).then_inc(s_made, 1)
            v.memset(xin[:, :, :], 0.0).then_inc(s_made, 1)
            link(v.memset(fill[:, :, :], 0))
            v.memset(fill_f[:, :, 1], 2.0 * P)
            v.memset(fill[:, :, 0], FAR).then_inc(s_zero, 1)
            dve.wait_ge(s_const, 1)
            link(v.tensor_copy(ramp[:, :], ramp_i))
            dve.wait_ge(s_src, 32)
            link(v.tensor_scalar(ramp_i[:, 0:COLS], src_sb[:, :], 7, None, ALU.arith_shift_right))
            v.tensor_copy(bins16[:, :], ramp_i[:, 0:COLS]).then_inc(s_recs, 1)
            link(v.tensor_scalar(src_sb[:, :], src_sb[:, :], P - 1, None, ALU.bitwise_and))
            v.tensor_copy(recs_f[:, :, 1], src_sb[:, :]).then_inc(s_recs, 1)
            dve.wait_ge(s_edge, 64)
            v.tensor_copy(recs[:, :, 0], dst_sb[:, :]).then_inc(s_recs, 1)
            v.tensor_copy(recs_f[:, :, 2], ew_sb[:, :]).then_inc(s_recs, 1)
            v.memset(recs[:, :, 3], 0).then_inc(s_recs, 1)
            dve.wait_ge(s_recs, 5)
            link(v.tensor_scalar(em8[:, :], ramp[:, 0:EXPERTS], float(EXPERTS), None, ALU.subtract))
            dve.wait_ge(s_const, 9)
            link(v.tensor_copy(ident16[:, :], ident[:, :]))
            v.sem_inc(s_cleared, 1)
            dve.wait_ge(s_par, 16 * 6)

            dve.wait_ge(s_numbers, 1)

            def one_hot(t, sub):
                cols = bins16[:, bass.ds(PER * t, PER)].unsqueeze(1).broadcast_to([P, BINS, PER])
                v.tensor_tensor(hot[:, sub, :, :], numbers[:, :, :], cols, ALU.is_equal).then_inc(s_hot, 1)

            def hist_step(i):
                for sub in range(2):
                    if not is_first(i):
                        dve.wait_ge(s_hist, 2 * i + sub - 1)
                    one_hot(2 * i + sub, sub)

            rounds(dve, NP_, hist_step)

            dve.wait_ge(s_hist, NT)
            for b in range(2):
                link(v.tensor_copy(totals[:, GRP * b:GRP * b + GRP, :], counts(b).rearrange("p b c -> p c b")))
            link(v.tensor_reduce(binsum[:, :], totals[:, :, :].rearrange("p c b -> p b c"), AX_X, ALU.add))
            link(v.tensor_scalar(binsum[:, :], binsum[:, :], float(P - 1), None, ALU.add))
            link(v.tensor_copy(bintile_i[:, :], binsum[:, :]))
            link(v.tensor_scalar(bintile_i[:, :], bintile_i[:, :], 7, None, ALU.arith_shift_right))
            link(v.tensor_copy(bintile[:, :], bintile_i[:, :]))
            link(v.tensor_tensor_scan(binend[:, :], onesf[:, 0:BINS], bintile[:, :], 0.0, ALU.mult, ALU.add))
            v.sem_inc(s_ends, 1)
            link(v.tensor_tensor(binsum[:, :], binend[:, :], bintile[:, :], ALU.subtract))
            link(v.tensor_scalar(base[:, 0, :], binsum[:, :], float(P), None, ALU.mult))
            for c in range(1, CHAINS):
                link(v.tensor_tensor(base[:, c, :], base[:, c - 1, :], totals[:, c - 1, :], ALU.add))
            link(v.memset(base[:, :, NT:BINS], BEYOND))
            v.sem_inc(s_base, 1)
            dve.wait_ge(s_colT, 1)
            link(v.tensor_copy(endcol[0:NT, :], bank[2][0:NT, 0:1]))
            v.tensor_scalar(past[0:NT, :], ramp[0:NT, :], endcol[0:NT, 0:1], None, ALU.is_ge).then_inc(s_past, 1)
            quarter = SLOTT // 4
            for q in range(4):
                dve.wait_ge(s_tbl, 4)
                v.tensor_scalar(tile_bin[0:1, q * quarter:(q + 1) * quarter], bank[3 + q][0:1, 0:quarter],
                                float(NT - 1), None, ALU.min).then_inc(s_tbl, 1)
            dve.wait_ge(s_based, 2)
            v.memset(rows[:, :, :], 0.0).then_inc(s_cleared, 1)

            def positions(i, sub):
                t = 2 * i + sub
                dve.wait_ge(s_red, GRPS * t + GRPS)
                v.tensor_copy(pos_i[:, sub, :], pos[:, sub, :]).then_inc(s_pos, 1)
                dve.wait_ge(s_pos, done(POS, "int", t))
                v.tensor_scalar(pos_row[:, sub, :], pos_i[:, sub, :], P - 1, None, ALU.bitwise_and).then_inc(s_pos, 1)
                v.tensor_scalar(pos_col[:, sub, :], pos_i[:, sub, :], 7, None, ALU.arith_shift_right).then_inc(s_pos, 1)
                dve.wait_ge(s_pos, done(POS, "col", t))
                if not is_first(i):
                    dve.wait_ge(s_scat[sub], 16 * PER * i)
                v.scalar_tensor_tensor(out=addr[:, sub, :], in0=pos_row[:, sub, :], scalar=float(SLOTT),
                                       in1=pos_col[:, sub, :], op0=ALU.mult, op1=ALU.add).then_inc(s_pos, 1)
                v.tensor_copy(rec_out[:, sub, :, :], recs[:, bass.ds(PER * t, PER), :]).then_inc(s_pos, 1)

            def held_aggr(s, sub, value):
                held(dve, "dve", s, value)
                v.bn_aggr(mv[:, sub, :], stats[:, sub, :]).then_inc(s, 1)

            def sort_step(i):
                for sub in range(2):
                    t = 2 * i + sub
                    s = s_ln_dve[sub]

                    def extract(gidx):
                        dve.wait_ge(s_rank, GRPS * t + gidx + 1)
                        v.tensor_tensor(prod[:, gidx % 2, :, :], hot_of(sub, gidx), counts(gidx % 2),
                                        ALU.mult).then_inc(s_read, 1)
                        dve.wait_ge(s_read, GRPS * t + gidx + 1)
                        v.tensor_reduce(pos[:, sub, GRP * gidx:GRP * gidx + GRP],
                                        prod[:, gidx % 2, :, :].rearrange("p b c -> p c b"),
                                        AX_X, ALU.add).then_inc(s_red, 1)

                    if not is_first(i):
                        dve.wait_ge(s_count, GRPS * (t - 1))
                    one_hot(t, sub)
                    dve.wait_ge(s_xin[sub], 16 * (i + 1))
                    v.bn_stats(stats[:, sub, :], xin[:, sub, :]).then_inc(s, 1)
                    v.tensor_tensor(acc[:, bass.ds(t, 1), :].rearrange("p a d -> p (a d)"), xin[:, sub, :],
                                    gb_sb[:, :], ALU.add)
                    extract(0)
                    held_aggr(s, sub, done(LN_DVE, "stats", i))
                    extract(1)
                    extract(2)
                    dve.wait_ge(s_ln_act[sub], done(LN_ACT, "std", i))
                    v.reciprocal(rstd[:, sub, :], std[:, sub, :]).then_inc(s, 1)
                    extract(3)
                    dve.wait_ge(s, done(LN_DVE, "rstd", i))
                    if not is_first(i):
                        dve.wait_ge(s_ln_pe[sub], done(LN_PE, "nT", i - 1))
                    v.tensor_scalar(normed[:, sub, :], xin[:, sub, :], mv[:, sub, 0:1], rstd[:, sub, 0:1],
                                    ALU.subtract, ALU.mult).then_inc(s, 1)
                    positions(i, sub)

            rounds(dve, NP_, sort_step)

            def make_pick(i, sub, k):
                n = PER * (2 * i + sub) + k
                if k == 0:
                    dve.wait_ge(s_recin[sub], 16 * (i + 1))
                if not (is_first(i) and sub == 0 and k < 4):
                    dve.wait_ge(s_sum, n - 3)
                v.tensor_scalar(pick[:, k % 4, :], ramp[:, 0:P], rec_in_f[:, sub, k, 1:2],
                                rec_in_f[:, sub, k, 2:3], ALU.is_equal, ALU.mult).then_inc(s_pick, 1)

            def add_sum(i, sub, k, where):
                n = PER * (2 * i + sub) + k
                place = acc[:, bass.ds(where, 1), :].rearrange("p a d -> p (a d)")
                dve.wait_ge(s_sum, n + 1)
                if not (is_first(i) and sub == 0 and k == 0):
                    dve.wait_ge(s_acc, n)
                v.tensor_tensor(place, place, bank[k % 4][:, 0:D], ALU.add).then_inc(s_acc, 1)

            def sum_step(i):
                for sub in range(2):
                    make_pick(i, sub, 0)
                    make_pick(i, sub, 1)
                    where = loads(dve, tile_bin[0:1, bass.ds(PER * (2 * i + sub), PER)], NT - 1)
                    for k in range(PER):
                        if k + 2 < PER:
                            make_pick(i, sub, k + 2)
                        add_sum(i, sub, k, where[k])

            dve.wait_ge(s_tbl, 8)
            dve.wait_ge(s_cleared, 2)
            rounds(dve, STEPS // 2, sum_step)

            dve.wait_ge(s_acc, SLOTT)

            def low_parts(i):
                dve.wait_ge(s_rt_act, done(RT_ACT, "high", i))
                v.tensor_tensor(pairs_out[:, :, D:HL], xn_rt, pairs_out[:, :, 0:D], ALU.subtract).then_inc(s_low, 1)

            def router_turn(i):
                def at(name):
                    return done(RT_DVE, name, i)

                def lanes(name, one):
                    for k in range(LANES):
                        last = one(k)
                    last.then_inc(s_rt_dve, 1)

                def x1_of(k):
                    return acc[:, bass.ds(LANES * i + k, 1), :].rearrange("p a d -> p (a d)")

                def stats_of(n, source):
                    if n == 2:
                        def one(k):
                            dve.wait_ge(s_y, LANES * i + k + 1)
                            return v.bn_stats(stats_rt[:, k, :], source(k))
                    else:
                        def one(k):
                            return v.bn_stats(stats_rt[:, k, :], source(k))
                    lanes(f"stats{n}", one)
                    held(dve, "dve", s_rt_dve, at(f"stats{n}"))
                    lanes(f"aggr{n}", lambda k: v.bn_aggr(mv_rt[:, k, :], stats_rt[:, k, :]))
                    if n == 2:
                        dve.wait_ge(s_rt_dve, at("aggr2"))

                def rstd_of(n):
                    dve.wait_ge(s_rt_act, done(RT_ACT, f"std{n}", i))
                    v.reciprocal(rstd_rt[:, :], std_rt[:, :]).then_inc(s_rt_dve, 1)
                    dve.wait_ge(s_rt_dve, at(f"rstd{n}"))

                stats_of(1, x1_of)
                if not is_first(i):
                    low_parts(i - 1)
                rstd_of(1)
                v.scalar_tensor_tensor(out=shift_rt[:, :], in0=mv_rt[:, :, 0], scalar=-1.0, in1=rstd_rt[:, :],
                                       op0=ALU.mult, op1=ALU.mult).then_inc(s_rt_dve, 1)
                stats_of(2, lambda k: y_rt[:, k, :])
                lanes("scaled", lambda k: v.scalar_tensor_tensor(
                    out=y_rt[:, k, :], in0=y_rt[:, k, :], scalar=mv_rt[:, k, 0:1], in1=gamma_sb[:, :],
                    op0=ALU.subtract, op1=ALU.mult))
                rstd_of(2)
                if not is_first(i):
                    dve.wait_ge(s_rtT_pe, LANES * i)
                lanes("xn", lambda k: v.scalar_tensor_tensor(
                    out=xn_rt[:, k, :], in0=y_rt[:, k, :], scalar=rstd_rt[:, k:k + 1], in1=beta_sb[:, :],
                    op0=ALU.mult, op1=ALU.add))

            rounds(dve, TURNS, router_turn)
            low_parts(TURNS - 1)

            def over_experts(ap):
                return ap.unsqueeze(2).broadcast_to([P, NT, EXPERTS])

            dve.wait_ge(s_lg_act, NT)
            numbers8 = em8[:, :].unsqueeze(1).broadcast_to([P, NT, EXPERTS])
            link(v.tensor_tensor(logits[:, :, :], logits[:, :, :],
                                 br_sb[:, :].unsqueeze(1).broadcast_to([P, NT, EXPERTS]), ALU.add))

            def largest(values, c, hot_c):
                link(v.tensor_reduce(vals[:, :, c], values, AX_X, ALU.max))
                link(v.tensor_tensor(hot_c, values, over_experts(vals[:, :, c]), ALU.is_equal))
                link(v.tensor_tensor(hot_c, hot_c, numbers8, ALU.mult))
                link(v.tensor_reduce(picked[:, :], hot_c, AX_X, ALU.min))
                link(v.tensor_tensor(hot_c, numbers8, over_experts(picked[:, :]), ALU.is_equal))

            largest(logits[:, :, :], 0, hot1)
            link(v.scalar_tensor_tensor(out=masked, in0=hot1, scalar=-HUGE, in1=logits[:, :, :],
                                        op0=ALU.mult, op1=ALU.add))
            largest(masked, 1, hot2)

            v.tensor_tensor(dn[:, :], vals[:, :, 1], vals[:, :, 0], ALU.subtract).then_inc(s_exp, 1)
            for hot_c in (hot1, hot2):
                link(v.tensor_scalar(hot_c[:, NT - 1, :], hot_c[:, NT - 1, :], valid[:, 0:1], None, ALU.mult))
            v.tensor_tensor(chosen[:, :, :], hot1[:, :, :], hot2[:, :, :], ALU.add).then_inc(s_ch, 1)
            dve.wait_ge(s_exp, 2)
            link(v.tensor_scalar(dn[:, :], den[:, :], 1.0, None, ALU.add))
            link(v.reciprocal(gate[:, :, 0], dn[:, :]))
            v.tensor_tensor(gate[:, :, 1], gate[:, :, 0], den[:, :], ALU.mult).then_inc(s_gate, 1)
            dve.wait_ge(s_chp, 1)
            hh = NT // 2
            for q in range(2):
                view = bank[2 + q][:, 0:hh * EXPERTS].rearrange("p (t e) -> p t e", e=EXPERTS)
                link(v.tensor_copy(texp[:, q * hh:(q + 1) * hh, :], view))
            for e in range(EXPERTS):
                v.tensor_tensor_scan(slot[:, :, e], onesf[:, 0:NT], texp[:, :, e], 0.0, ALU.mult, ALU.add)\
                    .then_inc(s_m2, 1)
            dve.wait_ge(s_m2, EXPERTS)
            link(v.tensor_scalar(ebase[:, :], slot[:, NT - 1, :], float(EROWS - 1), None, ALU.add))
            link(v.tensor_copy(etile_i[:, :], ebase[:, :]))
            link(v.tensor_scalar(etile_i[:, :], etile_i[:, :], 8, None, ALU.arith_shift_right))
            link(v.tensor_copy(etile[:, :], etile_i[:, :]))
            link(v.tensor_tensor_scan(eend[:, :], onesf[:, 0:EXPERTS], etile[:, :], 0.0, ALU.mult, ALU.add))
            v.sem_inc(s_ec, 1)
            link(v.tensor_tensor(ebase[:, :], eend[:, :], etile[:, :], ALU.subtract))
            link(v.tensor_scalar(ebase[:, :], ebase[:, :], float(EROWS), None, ALU.mult))
            link(v.tensor_tensor(slot[:, :, :], slot[:, :, :], texp[:, :, :], ALU.subtract))
            link(v.tensor_tensor(slot[:, :, :], slot[:, :, :],
                                 ebase[:, :].unsqueeze(1).broadcast_to([P, NT, EXPERTS]), ALU.add))
            for q in range(2):
                view = bank[q][:, 0:hh * EXPERTS].rearrange("p (t e) -> p t e", e=EXPERTS)
                part = slot[:, q * hh:(q + 1) * hh, :]
                link(v.tensor_tensor(part, part, view, ALU.add))
            for c, hot_c in enumerate((hot1, hot2)):
                link(v.tensor_tensor(texp[:, :, :], slot[:, :, :], hot_c[:, :, :], ALU.mult))
                link(v.tensor_reduce(slots_f[:, :, c], texp[:, :, :], AX_X, ALU.add))
            link(v.tensor_copy(slots[:, :, :], slots_f[:, :, :]))
            v.sem_inc(s_slots, 1)
            dve.wait_ge(s_ecs, 1)
            link(v.tensor_copy(endcol[0:EXPERTS, :], bank[6][0:EXPERTS, 0:1]))
            v.tensor_scalar(past[0:EXPERTS, 0:NE], ramp[0:EXPERTS, 0:NE], endcol[0:EXPERTS, 0:1], None,
                            ALU.is_ge).then_inc(s_etp, 1)
            dve.wait_ge(s_ecs, 2)
            v.tensor_scalar(tile_expert[:, :], bank[7][0:1, 0:NE], float(EXPERTS - 1), None, ALU.min)\
                .then_inc(s_etab, 1)

            def stage_slots(turn, b):
                return v.tensor_copy(slot_st[:, b, :, :], slots[:, bass.ds(LANES * turn, LANES), :])

            for b in range(2):
                stage_slots(b, b).then_inc(s_st_dve[b], 1)
            for e in range(EXPERTS):
                for n, (high, low) in enumerate(((w1h, w1l), (w2h, w2l))):
                    dve.wait_ge(s_whigh, 2 * e + n + 1)
                    v.scalar_tensor_tensor(out=low[:, e].rearrange("p k n -> p (k n)"), in0=w_in[:, e % 2, n, :],
                                           scalar=WSCALE, in1=high[:, e].rearrange("p k n -> p (k n)"),
                                           op0=ALU.mult, op1=ALU.subtract).then_inc(s_wlow, 1)

            def slots_turns(i):
                for b in range(2):
                    held(dve, "dve", s_disp[b], 32 * LANES * i)
                    stage_slots(2 * i + b, b).then_inc(s_st_dve[b], 1)

            with dve.Fori(1, TURNS // 2) as i:
                slots_turns(i)

            dve.wait_ge(s_wlow, 2 * EXPERTS)
            dve.wait_ge(s_b2, 16)
            dve.wait_ge(s_etab, 1)

            def expert_step(i):
                exp = loads(dve, tile_expert[0:1, bass.ds(2 * i, 2)], EXPERTS - 1)
                for sub in range(2):
                    for half in range(2):
                        part = slice(half * 2 * EROWS, (half + 1) * 2 * EROWS)
                        dve.wait_ge(s_ex_act[sub], done(EX_ACT, ("gelu_a", "gelu_b")[half], i))
                        v.tensor_copy(ex_hh[:, sub, part], ex_h[:, sub, part]).then_inc(s_ex_dve[sub], 1)
                        dve.wait_ge(s_ex_dve[sub], done(EX_DVE, ("high_a", "high_b")[half], i))
                        v.tensor_tensor(ex_hl[:, sub, part], ex_h[:, sub, part], ex_hh[:, sub, part],
                                        ALU.subtract).then_inc(s_ex_dve[sub], 1)
                for sub in range(2):
                    if not is_first(i):
                        dve.wait_ge(s_exst[sub], 16 * i)
                    dve.wait_ge(s_ex_pe[sub], done(EX_PE, "down", i))
                    v.scalar_tensor_tensor(
                        out=ex_y[:, sub], in0=bank[4 * sub + 3][:, :].rearrange("p (h n) -> p h n", h=2),
                        scalar=1.0 / WSCALE, in1=b2_sb[:, bass.ds(exp[sub], 1), :].broadcast_to([P, 2, D]),
                        op0=ALU.mult, op1=ALU.add).then_inc(s_ex_dve[sub], 1)

            rounds(dve, NE // 2, expert_step)

            dve.wait_ge(s_gate, 1)
            for b in range(2):
                dve.wait_ge(s_disp[b], 32 * LANES * (TURNS // 2))
                stage_slots(b, b).then_inc(s_cidx[b], 1)

            def combine_turns(i):
                for b in range(2):
                    turn = 2 * i + b
                    n = LANES * i
                    dve.wait_ge(s_cx[b], 16 * (i + 1))
                    dve.wait_ge(s_cg[b], 32 * LANES * (i + 1))
                    if not is_first(i):
                        dve.wait_ge(s_out[b], 16 * i)
                    for k in range(LANES):
                        v.scalar_tensor_tensor(out=x1_in[:, b, k, :], in0=got1[:, b, k, :],
                                               scalar=gate[:, bass.ds(LANES * turn + k, 1), 0],
                                               in1=x1_in[:, b, k, :], op0=ALU.mult, op1=ALU.add)\
                            .then_inc(s_cdve[b], 1)
                    dve.wait_ge(s_cdve[b], 2 * n + LANES)
                    for k in range(LANES):
                        v.scalar_tensor_tensor(out=summed[:, b, k, :], in0=got2[:, b, k, :],
                                               scalar=gate[:, bass.ds(LANES * turn + k, 1), 1],
                                               in1=x1_in[:, b, k, :], op0=ALU.mult, op1=ALU.add)\
                            .then_inc(s_cdve[b], 1)
                    if not is_last(i, TURNS // 2):
                        stage_slots(turn + 2, b).then_inc(s_cidx[b], 1)

            rounds(dve, TURNS // 2, combine_turns)


_INS = ['x', 'src', 'dst', 'edge_weight', 'L0_gnn_weight', 'L0_gnn_b', 'L0_ffn_gamma', 'L0_ffn_beta',
        'L0_ffn_Wr', 'L0_ffn_br', 'L0_ffn_W1', 'L0_ffn_b1', 'L0_ffn_W2', 'L0_ffn_b2']


def kernel(**inputs):
    import numpy as _np
    import concourse.bacc as _bacc
    from concourse import mybir as _mybir
    from concourse.bass_utils import run_bass_kernel_spmd as _run

    nc = _bacc.Bacc("TRN2", target_bir_lowering=False, num_devices=1)
    arrays, args = {}, []
    for name in _INS:
        a = _np.ascontiguousarray(inputs[name])
        arrays[f"in_{name}_dram"] = a
        args.append(nc.dram_tensor(f"in_{name}_dram", a.shape, _mybir.dt.from_np(a.dtype), kind="ExternalInput").ap())
    args.append(nc.dram_tensor("out_0_dram", (NODES, D), _mybir.dt.float32, kind="ExternalOutput").ap())
    gnn_moe(nc, *args)
    r = _run(nc, [arrays], core_ids=[0])
    return r.results[0]["out_0_dram"]
```

```python
from contextlib import ExitStack

import concourse.bass as bass
from concourse import mybir

F32 = mybir.dt.float32
I32 = mybir.dt.int32
BF16 = mybir.dt.bfloat16
F16 = mybir.dt.float16
ALU = mybir.AluOpType
ACT = mybir.ActivationFunctionType
AX_X = mybir.AxisListType.X

P = 128
NODES, D = 12500, 256
EDGES = 200000
EXPERTS, HID = 8, 512
EPS = 1e-5
NT = -(-NODES // P)
TAIL = NODES - (NT - 1) * P
KD, KH = D // P, HID // P
PER = 16
COLS = NT * PER
assert COLS * P >= EDGES
LAST = EDGES - (P - 1) * COLS
assert 0 < LAST <= COLS
BINS = NT + 1
GRP = 4
GRPS = PER // GRP
CHAINS = 2 * GRP
STEPS = -(-((EDGES + NT * (P - 1)) // P) // (2 * PER)) * 2
SLOTT = STEPS * PER
NSLOT = SLOTT * P
FAR = 1 << 20
BEYOND = float(1 << 25)
EROWS = 2 * P
NE = (2 * NODES + EXPERTS * (EROWS - 1)) // EROWS
NE += NE % 2
FILLS = 16
ECAP = (-(-NODES // EROWS) + 1) * EROWS
ZERO_AT = EXPERTS * ECAP
COPIES = 4
assert NODES % COPIES == 0
LANES = 7
TURNS = NT // LANES
assert TURNS * LANES == NT and TURNS % 2 == 0
SPLITS = EXPERTS // 2
HL = 2 * D
NOTE = 4
ROW = HL // 2 + NOTE
WSCALE = 64.0
HUGE = 3.0e38


def done(steps, name, i):
    return i * len(steps) + steps.index(name) + 1


def rounds(eng, n, body):
    body(0)
    with eng.Fori(1, n - 1) as i:
        body(i)
    body(n - 1)


def is_first(i):
    return isinstance(i, int) and i == 0


def is_last(i, n):
    return isinstance(i, int) and i == n - 1


LN_DVE = ("stats", "aggr", "rstd", "norm")
LN_ACT = ("std", "nT", "h")
LN_PE = ("nT", "h")
POS = ("int", "row", "col", "addr", "rec")
RT_DVE = ("stats", "aggr", "rstd", "shift", "scaled", "xn")
RT_ACT = ("std", "high")
TOP = ("logits", "max1", "equal1", "number1", "first1", "hot1", "masked",
       "max2", "equal2", "number2", "first2", "hot2", "chosen")
PLACE = ("slot", "taken", "own", "sum", "int")
GATES = ("node", "next", "first", "total", "gate1", "gate2")
EX_PE = ("up_a", "up_b", "down")
EX_ACT = ("gelu_a", "gelu_b")
EX_DVE = ("high_a", "low_a", "high_b", "low_b", "y", "gated")


def gnn_moe(nc, x, src, dst, edge_weight, gw, gb, gamma, beta, wr, br, w1, b1, w2, b2, out):
    h_rows = nc.dram_tensor("h_rows", (NT * P, D), F32).ap()
    edges_sorted = nc.dram_tensor("edges_sorted", (NSLOT, 4), I32).ap()
    expert_in = nc.dram_tensor("expert_in", (ZERO_AT + EROWS, ROW), I32).ap()

    weight_pairs = nc.dram_tensor("weight_pairs", (EXPERTS, P, 4 * KD * HID), F16).ap()
    sums = nc.dram_tensor("sums", (NT * P + EROWS, D), F32).ap()

    with ExitStack() as ctx:
        def sb(name, shape, dt=F32):
            return ctx.enter_context(nc.sbuf_tensor(name, shape, dt))

        def sem(name):
            return ctx.enter_context(nc.semaphore(name))

        def sem2(name):
            return [sem(f"{name}{i}") for i in range(2)]

        acc = sb("acc", [P, NT, D])
        flat = acc[:, :, :].rearrange("p t d -> p (t d)")
        wsize = 2 * KD * HID
        split = flat[:, 0:EXPERTS * wsize].bitcast(F16).rearrange("p (e w m) -> p e w m", e=EXPERTS, w=4)
        w1h, w1l = (split[:, :, k, :].rearrange("p e (k n) -> p e k n", k=KD) for k in range(2))
        w2h, w2l = (split[:, :, k, :].rearrange("p e (k n) -> p e k n", k=KH) for k in range(2, 4))
        b2_sb = flat[:, EXPERTS * wsize:EXPERTS * (wsize + D)].rearrange("p (e n) -> p e n", e=EXPERTS)
        assert EXPERTS * (wsize + D) <= (TURNS - 2) * LANES * D

        def turns_of(words):
            return -(-words // (LANES * D))

        made_at = NT * D - 2 * wsize
        made = flat[:, made_at:NT * D].bitcast(F16).rearrange("p (b w m) -> p b w m", b=2, w=4)
        assert made_at >= 2 * (SPLITS + 1) * D

        recs = sb("recs", [P, COLS, 4], I32)
        recs_f = recs[:, :, :].bitcast(F32)
        bins16 = sb("bins16", [P, COLS], BF16)
        src_sb, dst_sb = (flat[:, k * COLS:(k + 1) * COLS].bitcast(I32) for k in range(2))
        ew_sb = flat[:, 2 * COLS:3 * COLS]
        ramp_i = flat[:, 3 * COLS:3 * COLS + SLOTT].bitcast(I32)
        late = recs_f.rearrange("p t w -> p (t w)")
        y_rt = late[:, 0:2 * LANES * D].rearrange("p (b s n) -> p b s n", b=2, s=LANES)
        xnT_rt = late[:, 2 * LANES * D:3 * LANES * D].rearrange("p (s n) -> p s n", s=LANES)
        stats_at = 3 * LANES * D
        rstd_x1, shift_x1 = (late[:, stats_at + k * NT:stats_at + (k + 1) * NT] for k in range(2))
        ended = late[0:1, stats_at:stats_at + NE * EXPERTS].rearrange("p (j e) -> p j e", e=EXPERTS)
        ex_xT = late[:, 0:4 * EROWS].bitcast(F16).rearrange("p (s n) -> p s n", s=2)
        ex_hh, ex_hl = (late[:, 4 * EROWS * (1 + k):4 * EROWS * (2 + k)].bitcast(F16)
                        .rearrange("p (s n) -> p s n", s=2) for k in range(2))
        ex_row = late[:, 12 * EROWS:12 * EROWS + 4 * ROW].rearrange("p (s h n) -> p s h n", s=2, h=2)
        ex_words, ex_x = (late[:, 12 * EROWS:12 * EROWS + 4 * ROW].bitcast(dt)
                          .rearrange("p (s h n) -> p s h n", s=2, h=2) for dt in (I32, F16))
        assert 12 * EROWS + 4 * ROW <= stats_at
        fill = sb("fill", [P, SLOTT // FILLS, 4], I32)
        fill_f = fill[:, :, :].bitcast(F32)
        ramp = sb("ramp", [P, SLOTT])
        past = sb("past", [P, SLOTT], BF16)
        empty = sb("empty", [P, EROWS // P, ROW], I32)
        spare = sb("spare", [P, EROWS // P])
        tri = sb("tri", [P, P], BF16)
        rest = sb("rest", [P, P], BF16)
        ones = sb("ones", [P, P], BF16)
        onesf = sb("onesf", [P, P])
        ident = sb("ident", [P, P])
        ident16 = sb("ident16", [P, P], F16)
        valid = sb("valid", [P, 1])
        eps = sb("eps", [P, 1])
        gw_sb = sb("gw_sb", [P, KD, D])
        gb_sb = sb("gb_sb", [P, D])
        gamma_sb = sb("gamma_sb", [P, D])
        beta_sb = sb("beta_sb", [P, D])
        wr_sb = sb("wr_sb", [P, KD, EXPERTS])
        br_sb = sb("br_sb", [P, EXPERTS])
        one_hots = BINS * PER // 2
        work = sb("work", [P, 3 * one_hots + 2 * BINS * GRP])
        hot = work[:, 0:2 * one_hots].bitcast(BF16).rearrange("p (s b c) -> p s b c", s=2, b=BINS)
        numbers = work[:, 2 * one_hots:3 * one_hots].bitcast(BF16).rearrange("p (b c) -> p b c", b=BINS)
        prod = work[:, 3 * one_hots:3 * one_hots + 2 * BINS * GRP].rearrange("p (s b c) -> p s b c", s=2, b=BINS)
        rows = sb("rows", [P, PER, D])
        rows_flat = rows[:, :, :].rearrange("p k d -> p (k d)")
        w_in = rows_flat[:, 0:4 * KD * HID].rearrange("p (b w n) -> p b w n", b=2, w=2)
        pairs = rows_flat[:, 0:2 * LANES * ROW].bitcast(F16).rearrange("p (b s n) -> p b s n", b=2, s=LANES)
        notes = rows_flat[:, 0:2 * LANES * ROW].rearrange("p (b s n) -> p b s n", b=2, s=LANES)[:, :, :, D:ROW]
        row_words = rows_flat[:, 0:2 * LANES * ROW].bitcast(I32).rearrange("p (b s n) -> p b s n", b=2, s=LANES)
        ex_h = rows_flat[:, 0:8 * EROWS].rearrange("p (s n) -> p s n", s=2)
        ex_y = rows_flat[:, 8 * EROWS:12 * EROWS].rearrange("p (s h n) -> p s h n", s=2, h=2)
        hist_hot = [hot[:, k] for k in range(2)] + [
            rows_flat[:, k * one_hots:(k + 1) * one_hots].bitcast(BF16).rearrange("p (b c) -> p b c", b=BINS)
            for k in range(LANES - 2)]
        totals, base = (rows_flat[:, k * CHAINS * BINS:(k + 1) * CHAINS * BINS]
                        .rearrange("p (c b) -> p c b", c=CHAINS) for k in range(2))
        binsum = sb("binsum", [P, BINS])
        bintile_i = sb("bintile_i", [P, BINS], I32)
        bintile = sb("bintile", [P, BINS])
        binend = sb("binend", [P, BINS])
        endcol = sb("endcol", [P, 1])
        tile_bin = sb("tile_bin", [1, SLOTT], I32)
        pos = sb("pos", [P, 2, PER])
        pos_i = sb("pos_i", [P, 2, PER], I32)
        pos_row = sb("pos_row", [P, 2, PER], I32)
        pos_col = sb("pos_col", [P, 2, PER], I32)
        addr = sb("addr", [P, 2, PER], I32)
        rec_out = sb("rec_out", [P, 2, PER, 4], I32)
        xin = sb("xin", [P, 2, D])
        stats = sb("stats", [P, 2, 6])
        mv = sb("mv", [P, 2, 2])
        std = sb("std", [P, 2, 1])
        rstd = sb("rstd", [P, 2, 1])
        normed = sb("normed", [P, 2, D])
        normedT = sb("normedT", [P, 2, D])
        h_out = sb("h_out", [P, 2, D])
        rec_in = sb("rec_in", [P, 2, PER, 4], I32)
        rec_in_f = rec_in[:, :, :, :].bitcast(F32)
        pick = sb("pick", [P, 4, P])
        stats_rt = sb("stats_rt", [P, LANES, 6])
        mv_rt = sb("mv_rt", [P, LANES, 2])
        std_rt = sb("std_rt", [P, LANES])
        stats_2 = sb("stats_2", [P, 2 * LANES, 6])
        mv_2 = sb("mv_2", [P, 2 * LANES, 2])
        std_2 = sb("std_2", [P, 2 * LANES])
        rstd_2 = sb("rstd_2", [P, 2 * LANES])
        rstd_rt = sb("rstd_rt", [P, LANES])
        shift_rt = sb("shift_rt", [P, LANES])
        em8 = sb("em8", [P, EXPERTS])
        b1_rows = sb("b1_rows", [EXPERTS * KH, P])
        b1T = sb("b1T", [P, EXPERTS * KH])
        logits = sb("logits", [P, LANES, EXPERTS])
        masked = sb("masked", [P, LANES, EXPERTS])
        hots = sb("hots", [P, 2, LANES, EXPERTS])
        vals = sb("vals", [P, 2, LANES])
        first = sb("first", [P, 2, LANES])
        node = sb("node", [P, LANES])
        chosen = sb("chosen", [P, LANES + 1, EXPERTS], BF16)
        slot = sb("slot", [P, LANES, EXPERTS])
        own = sb("own", [P, 2, LANES, EXPERTS])
        own_slot = sb("own_slot", [P, 2, LANES])
        taken = sb("taken", [P, EXPERTS])
        taken_i = sb("taken_i", [1, EXPERTS], I32)
        slot_st = sb("slot_st", [P, 2, 2, LANES], I32)
        note = sb("note", [P, 2, 2, NOTE])
        is_top = sb("is_top", [P, 2, 2])
        gate_top = sb("gate_top", [P, 2, 2])
        gate_second = sb("gate_second", [P, 2, 2])
        gate = sb("gate", [P, 2, 2])
        ex_node = sb("ex_node", [P, 2, 2])
        node_st = sb("node_st", [P, 2, 2], I32)
        gap = sb("gap", [P, EXPERTS])
        count = sb("count", [P, EXPERTS])
        etile_i = sb("etile_i", [P, EXPERTS], I32)
        etile = sb("etile", [P, EXPERTS])
        eend = sb("eend", [P, EXPERTS])
        tile_sum = sb("tile_sum", [1, NE])
        tile_expert = sb("tile_expert", [1, NE], I32)
        tile_block = sb("tile_block", [1, NE], I32)
        less = sb("less", [P, LANES])
        ratio = sb("ratio", [P, LANES])
        total = sb("total", [P, LANES])

        bank = [ctx.enter_context(nc.psum_tensor(f"bank{i}", [P, 512], F32)) for i in range(8)]
        NG = GRP * BINS
        assert NG <= 512

        def counts(b):
            return bank[b][:, 0:NG].rearrange("p (b c) -> p b c", c=GRP)

        def hot_of(sub, gidx):
            return hot[:, sub, :, GRP * gidx:GRP * gidx + GRP]

        s_src, s_edge, s_par = sem("s_src"), sem("s_edge"), sem("s_par")
        s_const, s_made, s_recs = sem("s_const"), sem("s_made"), sem("s_recs")
        s_fill, s_zero, s_zeroed = sem("s_fill"), sem("s_zero"), sem("s_zeroed")
        s_stats, s_scale, s_stdx, s_rstdx = (sem(n) for n in ("s_stats", "s_scale", "s_stdx", "s_rstdx"))
        s_gates, s_note, s_pass = sem("s_gates"), sem2("s_note"), sem("s_pass")
        s_wst, s_wback = sem("s_wst"), sem("s_wback")
        s_less, s_ratio, s_z = sem("s_less"), sem("s_ratio"), sem("s_z")
        s_top, s_place, s_prefix, s_valid, s_tail = (sem(n) for n in (
            "s_top", "s_place", "s_prefix", "s_valid", "s_tail"))
        s_hot, s_hist = sem("s_hot"), sem("s_hist")
        s_mid, s_base, s_based, s_colT, s_ends, s_tbl = (sem(n) for n in (
            "s_mid", "s_base", "s_based", "s_colT", "s_ends", "s_tbl"))
        s_rank, s_read, s_count, s_red, s_pos = (sem(n) for n in (
            "s_rank", "s_read", "s_count", "s_red", "s_pos"))
        s_scat = sem2("s_scat")
        s_xin, s_ln_dve, s_ln_act, s_ln_pe, s_hst = (sem2(n) for n in (
            "s_xin", "s_ln_dve", "s_ln_act", "s_ln_pe", "s_hst"))
        s_recin = sem2("s_recin")
        s_row = [sem(f"s_row{k}") for k in range(PER)]
        s_pick, s_sum, s_acc = sem("s_pick"), sem("s_sum"), sem("s_acc")
        s_rt_dve, s_rt_act, s_rtT_pe, s_rtT_act, s_lg_pe, s_x1st = (sem(n) for n in (
            "s_rt_dve", "s_rt_act", "s_rtT_pe", "s_rtT_act", "s_lg_pe", "s_x1st"))
        s_y, s_low = sem("s_y"), sem("s_low")
        s_b1, s_b1T, s_b1c, s_b2 = sem("s_b1"), sem("s_b1T"), sem("s_b1c"), sem("s_b2")
        s_past, s_etab = sem("s_past"), sem("s_etab")
        s_disp = sem2("s_disp")
        s_win, s_whigh, s_wlow = sem2("s_win"), sem("s_whigh"), sem("s_wlow")
        s_exin, s_ex_pe, s_ex_act, s_ex_dve, s_exst = (
            sem2("s_exin"), sem2("s_ex_pe"), sem2("s_ex_act"), sem2("s_ex_dve"), sem2("s_exst"))
        s_exT_pe, s_exT_act = sem2("s_exT_pe"), sem2("s_exT_act")
        s_numbers = sem("s_numbers")
        s_cleared, s_out = sem("s_cleared"), sem("s_out")
        s_held = {n: sem(f"s_held_{n}") for n in ("pool", "act", "dve")}

        def held(eng, which, s, value):
            eng.wait_ge(s, value)
            eng.sem_inc(s_held[which], 1)

        def loads(eng, ap, top):
            return nc.values_load_multi_w_load_instructions(
                ap, engines=(eng.engine,), min_val=0, max_val=top, skip_runtime_bounds_check_because="a table of the program's own")[1]

        x_rows = x
        NP_ = NT // 2
        lane_banks = (LANES + 1) // 2
        assert NT % 2 == 0 and STEPS % 2 == 0

        block = ctx.enter_context(nc.Block())

        @block.sync
        def _(sp):
            def spread(ap, dst_sb, s):
                full = (P - 1) * COLS
                sp.dma_start(dst_sb[0:P - 1, :], ap[0:full].rearrange("(p t) -> p t", t=COLS)).then_inc(s, 16)
                sp.dma_start(dst_sb[P - 1:P, 0:LAST], ap[full:EDGES].rearrange("(p t) -> p t", p=1)).then_inc(s, 16)

            sp.wait_ge(s_made, 3)
            spread(src, src_sb, s_src)
            spread(dst, dst_sb, s_edge)
            spread(edge_weight, ew_sb, s_edge)
            sp.dma_start(gw_sb[:, :, :], gw.rearrange("(k p) n -> p k n", p=P)).then_inc(s_par, 16)
            sp.dma_start(wr_sb[:, :, :], wr.rearrange("(k p) n -> p k n", p=P)).then_inc(s_par, 16)
            sp.dma_start(b1_rows[:, :], b1.rearrange("e (c p) -> (e c) p", p=P)).then_inc(s_b1, 16)
            for ap, t in ((gb, gb_sb), (gamma, gamma_sb), (beta, beta_sb), (br, br_sb)):
                sp.dma_start(t[:, :], ap.partition_broadcast(P)).then_inc(s_par, 16)
            sp.wait_ge(s_zero, 2)
            part = SLOTT // FILLS
            grid = edges_sorted.rearrange("(p t) w -> p t w", p=P)
            for k in range(FILLS):
                sp.dma_start(grid[:, k * part:(k + 1) * part, :], fill[:, :, :]).then_inc(s_fill, 16)
            sp.dma_start(expert_in[ZERO_AT:ZERO_AT + EROWS, :].rearrange("(p t) d -> p (t d)", p=P),
                         empty[:, :, :].rearrange("p t d -> p (t d)")).then_inc(s_zeroed, 16)

            def node_tile(i):
                for sub in range(2):
                    t = 2 * i + sub
                    n = TAIL if is_last(i, NP_) and sub else P
                    if not is_first(i):
                        sp.wait_ge(s_ln_dve[sub], done(LN_DVE, "norm", i - 1))
                    sp.dma_start(xin[0:n, sub, :], x_rows[bass.ds(t * P, n), :]).then_inc(s_xin[sub], 16)
                for sub in range(2):
                    t = 2 * i + sub
                    sp.wait_ge(s_ln_act[sub], done(LN_ACT, "h", i))
                    sp.dma_start(h_rows[bass.ds(t * P, P), :], h_out[:, sub, :]).then_inc(s_hst[sub], 16)

            rounds(sp, NP_, node_tile)

            for sub in range(2):
                sp.wait_ge(s_scat[sub], 16 * PER * NP_)

            def sorted_step(i):
                for sub in range(2):
                    step = 2 * i + sub
                    if not is_first(i):
                        sp.wait_ge(s_sum, PER * (step - 1))
                    sp.dma_start(rec_in[:, sub, :, :],
                                 grid[:, bass.ds(step * PER, PER), :]).then_inc(s_recin[sub], 16)

            rounds(sp, STEPS // 2, sorted_step)

            sums_grid = sums[0:NT * P, :].rearrange("(t p) d -> p t d", p=P)
            sp.wait_ge(s_acc, SLOTT)
            for k in range(LANES):
                sp.dma_start(sums_grid[:, k * TURNS:(k + 1) * TURNS, :],
                             acc[:, k * TURNS:(k + 1) * TURNS, :]).then_inc(s_x1st, 16)
            sp.dma_start(sums[NT * P:NT * P + EROWS, :].rearrange("(p t) d -> p t d", p=P),
                         empty[:, :, 0:D].bitcast(F32)).then_inc(s_x1st, 16)

            sp.wait_ge(s_x1st, 16 * (LANES + 1))
            sp.wait_ge(s_wst, 16 * EXPERTS)
            for e in range(EXPERTS):
                sp.wait_ge(s_y, LANES * turns_of((e + 1) * wsize))
                sp.dma_start(flat[:, e * wsize:(e + 1) * wsize].bitcast(F16), weight_pairs[e]).then_inc(s_wback, 16)
            sp.wait_ge(s_y, LANES * turns_of(EXPERTS * (wsize + D)))
            sp.dma_start(b2_sb, b2.partition_broadcast(P)).then_inc(s_b2, 16)

            sp.wait_ge(s_tail, 1)
            tails = loads(sp, taken_i[0:1, :], ZERO_AT - EROWS)
            for e in range(EXPERTS):
                sp.dma_start(expert_in[bass.ds(tails[e], EROWS), :].rearrange("(p t) d -> p (t d)", p=P),
                             empty[:, :, :].rearrange("p t d -> p (t d)")).then_inc(s_zeroed, 16)

            for b in range(2):
                sp.wait_ge(s_disp[b], 32 * LANES * (TURNS // 2))
            sp.wait_ge(s_zeroed, 16 * (EXPERTS + 1))
            sp.wait_ge(s_etab, 1)
            in_grid = expert_in.rearrange("(t h p) d -> p t h d", p=P, h=2)

            def load_rows(i, sub):
                block_at = loads(sp, tile_block[0:1, bass.ds(2 * i + sub, 1)], ZERO_AT // EROWS)[0]
                sp.dma_start(ex_words[:, sub], in_grid[:, bass.ds(block_at, 1), :, :]
                             .rearrange("p a h d -> p (a h) d")).then_inc(s_exin[sub], 16)

            for sub in range(2):
                load_rows(0, sub)

            def expert_step(i):
                if not is_last(i, NE // 2):
                    for sub in range(2):
                        sp.wait_ge(s_exT_pe[sub], i + 1)
                        sp.wait_ge(s_note[sub], i + 1)
                        load_rows(i + 1, sub)

            rounds(sp, NE // 2, expert_step)

            for sub in range(2):
                sp.wait_ge(s_exst[sub], 32 * (NE // 2))
            part = NODES // COPIES
            for k in range(COPIES):
                sp.dma_start(out[k * part:(k + 1) * part, :], sums[k * part:(k + 1) * part, :]).then_inc(s_out, 16)
            sp.wait_ge(s_out, 16 * COPIES)

        @block.gpsimd
        def _(pool):
            g = nc.gpsimd
            g.iota(ramp_i, [[1, SLOTT]], base=0, channel_multiplier=0).then_inc(s_const, 1)
            g.iota(numbers[:, :, :], [[1, BINS], [0, PER]], base=0, channel_multiplier=0,
                   allow_small_or_imprecise_dtypes=True).then_inc(s_numbers, 1)
            g.memset(tri[:, :], 1.0).then_inc(s_const, 1)
            g.memset(rest[:, :], 1.0).then_inc(s_const, 1)
            g.memset(ident[:, :], 0.0).then_inc(s_const, 1)
            g.memset(valid[:, :], 1.0).then_inc(s_const, 1)
            pool.wait_ge(s_const, 5)
            g.affine_select(out=tri[:, :], in_=tri[:, :], compare_op=ALU.is_gt, fill=0.0, base=0,
                            pattern=[[1, P]], channel_multiplier=-1).then_inc(s_const, 1)
            g.affine_select(out=rest[:, :], in_=rest[:, :], compare_op=ALU.is_ge, fill=0.0, base=0,
                            pattern=[[-1, P]], channel_multiplier=1).then_inc(s_const, 1)
            g.affine_select(out=ident[:, :], in_=ident[:, :], compare_op=ALU.not_equal, fill=1.0, base=0,
                            pattern=[[-1, P]], channel_multiplier=1).then_inc(s_const, 1)
            g.affine_select(out=valid[:, :], in_=valid[:, :], compare_op=ALU.is_ge, fill=0.0, base=TAIL - 1,
                            pattern=[[0, 1]], channel_multiplier=-1).then_inc(s_const, 1)
            g.iota(spare[:, :], [[1, EROWS // P]], base=NT * P, channel_multiplier=EROWS // P,
                   allow_small_or_imprecise_dtypes=True).then_inc(s_numbers, 1)
            g.iota(node[:, :], [[P, LANES]], base=0, channel_multiplier=1,
                   allow_small_or_imprecise_dtypes=True).then_inc(s_numbers, 1)

            pool.wait_ge(s_fill, 16 * FILLS)

            def scatter_step(i):
                for sub in range(2):
                    held(pool, "pool", s_pos, done(POS, "rec", 2 * i + sub))
                    for k in range(PER):
                        pool.indirect_dma_start(
                            out=edges_sorted[:, :],
                            out_offset=bass.IndirectOffsetOnAxis(ap=addr[:, sub, k:k + 1], axis=0),
                            in_=rec_out[:, sub, k, :], in_offset=None,
                            bounds_check=NSLOT - 1, oob_is_err=False).then_inc(s_scat[sub], 16)

            rounds(pool, NP_, scatter_step)

            pool.wait_ge(s_cleared, 2)
            for sub in range(2):
                pool.wait_ge(s_hst[sub], 16 * NP_)

            def gather_step(i):
                for sub in range(2):
                    step = 2 * i + sub
                    held(pool, "pool", s_recin[sub], 16 * (i + 1))
                    for k in range(PER):
                        if k % 4 == 0 and not (is_first(i) and sub == 0):
                            held(pool, "pool", s_sum, PER * step - PER + k + 4)
                        pool.indirect_dma_start(
                            out=rows[:, k, :], out_offset=None, in_=h_rows[:, :],
                            in_offset=bass.IndirectOffsetOnAxis(ap=rec_in[:, sub, k, 0:1], axis=0),
                            bounds_check=NODES - 1, oob_is_err=False).then_inc(s_row[k], 16)

            rounds(pool, STEPS // 2, gather_step)

            def dispatch_turns(i):
                for b in range(2):
                    turn = 2 * i + b
                    held(pool, "pool", s_low, turn + 1)
                    held(pool, "pool", s_gates, done(GATES, "gate2", turn))
                    for k in range(LANES):
                        n = TAIL if is_last(i, TURNS // 2) and b and k == LANES - 1 else P
                        for c in range(2):
                            pool.indirect_dma_start(
                                out=expert_in[:, :],
                                out_offset=bass.IndirectOffsetOnAxis(ap=slot_st[0:n, b, c, k:k + 1], axis=0),
                                in_=row_words[0:n, b, k, :], in_offset=None,
                                bounds_check=ZERO_AT - 1, oob_is_err=False).then_inc(s_disp[b], 16)

            rounds(pool, TURNS // 2, dispatch_turns)

            pool.wait_ge(s_x1st, 16 * (LANES + 1))

            def add_step(i):
                for sub in range(2):
                    held(pool, "pool", s_ex_dve[sub], done(EX_DVE, "gated", i))
                    if sub:
                        held(pool, "pool", s_exst[0], 32 * (i + 1))
                    elif not is_first(i):
                        held(pool, "pool", s_exst[1], 32 * i)
                    for h in range(2):
                        pool.indirect_dma_start(
                            out=sums[:, :], out_offset=bass.IndirectOffsetOnAxis(ap=node_st[:, sub, h:h + 1], axis=0),
                            in_=ex_y[:, sub, h, :], in_offset=None, compute_op=ALU.add).then_inc(s_exst[sub], 16)

            rounds(pool, NE // 2, add_step)

        @block.tensor
        def _(pe):
            mm = nc.tensor.matmul
            pe.wait_ge(s_made, 7)
            pe.wait_ge(s_const, 9)

            def hist_step(i):
                for k, tile_hot in enumerate(hist_hot):
                    pe.wait_ge(s_hot, LANES * i + k + 1)
                    for gidx in range(GRPS):
                        last = mm(counts(gidx % 2), ones[:, :], tile_hot[:, :, GRP * gidx:GRP * gidx + GRP],
                                  start=is_first(i) and k == 0 and gidx < 2,
                                  stop=is_last(i, TURNS) and k == LANES - 1 and gidx >= GRPS - 2,
                                  skip_group_check=True)
                    last.then_inc(s_hist, 1)

            rounds(pe, TURNS, hist_step)

            pe.wait_ge(s_ends, 1)
            mm(bank[2][0:NT, 0:1], binend[0:1, 0:NT], onesf[0:1, 0:1], start=True, stop=True).then_inc(s_colT, 1)
            pe.wait_ge(s_base, 1)
            for b in range(2):
                mm(counts(b), onesf[0:1, :], base[0:1, GRP * b:GRP * b + GRP, :].rearrange("p c b -> p b c"), start=True, stop=False,
                   skip_group_check=True).then_inc(s_based, 1)
            pe.wait_ge(s_past, 1)
            quarter = SLOTT // 4
            for q in range(4):
                mm(bank[3 + q][0:1, 0:quarter], ones[0:NT, 0:1], past[0:NT, q * quarter:(q + 1) * quarter],
                   start=True, stop=True).then_inc(s_tbl, 1)
            pe.wait_ge(s_tbl, 8)

            def rank(t, sub, gidx):
                if gidx == 0:
                    pe.wait_ge(s_hot, t + (NT + 1))
                mm(counts(gidx % 2), tri[:, :], hot_of(sub, gidx), start=False, stop=False,
                   skip_group_check=True).then_inc(s_rank, 1)

            def count(t, sub, gidx):
                pe.wait_ge(s_read, GRPS * t + gidx + 1)
                mm(counts(gidx % 2), rest[:, :], hot_of(sub, gidx), start=False, stop=False,
                   skip_group_check=True).then_inc(s_count, 1)

            def ln_T(i, sub):
                pe.wait_ge(s_ln_dve[sub], done(LN_DVE, "norm", i))
                for k in range(KD):
                    last = nc.tensor.transpose(bank[2 + sub][:, k * P:(k + 1) * P],
                                               normed[:, sub, k * P:(k + 1) * P], ident[:, :])
                last.then_inc(s_ln_pe[sub], 1)

            def ln_h(i, sub):
                pe.wait_ge(s_ln_act[sub], done(LN_ACT, "nT", i))
                for k in range(KD):
                    last = mm(bank[4 + sub][:, 0:D], normedT[:, sub, k * P:(k + 1) * P], gw_sb[:, k, :],
                              start=(k == 0), stop=(k == KD - 1))
                last.then_inc(s_ln_pe[sub], 1)

            pe.wait_ge(s_b1, 16)
            nc.tensor.transpose(bank[7][:, 0:EXPERTS * KH], b1_rows[:, :], ident[0:EXPERTS * KH, 0:EXPERTS * KH])\
                .then_inc(s_b1T, 1)
            pe.wait_ge(s_par, 16 * 6)

            def sort_step(i):
                for sub in range(2):
                    t = 2 * i + sub
                    rank(t, sub, 0)
                    rank(t, sub, 1)
                    count(t, sub, 0)
                    rank(t, sub, 2)
                    count(t, sub, 1)
                    rank(t, sub, 3)
                    count(t, sub, 2)
                    count(t, sub, 3)
                    if sub == 0:
                        ln_T(i, 0)
                ln_h(i, 0)
                ln_T(i, 1)
                ln_h(i, 1)

            rounds(pe, NP_, sort_step)

            for sub in range(2):
                pe.wait_ge(s_ln_act[sub], done(LN_ACT, "h", NP_ - 1))

            def sum_step(i):
                for sub in range(2):
                    for k in range(PER):
                        n = PER * (2 * i + sub) + k
                        pe.wait_ge(s_pick, n + 1)
                        pe.wait_ge(s_row[k], 16 * (2 * i + sub + 1))
                        if not (is_first(i) and sub == 0 and k < 4):
                            pe.wait_ge(s_acc, n - 3)
                        mm(bank[k % 4][:, 0:D], pick[:, k % 4, :], rows[:, k, :],
                           start=True, stop=True).then_inc(s_sum, 1)

            rounds(pe, STEPS // 2, sum_step)

            def router_turns(i):
                for b in range(2):
                    turn = 2 * i + b
                    pe.wait_ge(s_rt_dve, done(RT_DVE, "xn", turn))
                    for k in range(LANES):
                        for c in range(KD):
                            at = (k % 2 * KD + c) * P
                            last = nc.tensor.transpose(bank[k // 2][:, at:at + P],
                                                       y_rt[:, b, k, c * P:(c + 1) * P], ident[:, :])
                        if k % 2 or k == LANES - 1:
                            last.then_inc(s_rtT_pe, 1)
                    for k in range(LANES):
                        if k % 2 == 0:
                            pe.wait_ge(s_rtT_act, lane_banks * turn + k // 2 + 1)
                        for c in range(KD):
                            last = mm(bank[4][:, k * EXPERTS:(k + 1) * EXPERTS], xnT_rt[:, k, c * P:(c + 1) * P],
                                      wr_sb[:, c, :], start=(c == 0), stop=(c == KD - 1))
                    last.then_inc(s_lg_pe, 1)
                    pe.wait_ge(s_top, done(TOP, "chosen", turn))
                    ch = chosen[:, :, :].rearrange("p t e -> p (t e)")
                    wide = (LANES + 1) * EXPERTS
                    mm(bank[5][:, 0:wide], tri[:, :], ch, start=True, stop=False, skip_group_check=True)
                    for k in range(1, LANES + 1):
                        last = mm(bank[5][:, k * EXPERTS:wide], ones[:, :], ch[:, 0:wide - k * EXPERTS],
                                  start=False, stop=k == LANES, skip_group_check=True)
                    last.then_inc(s_prefix, 1)

            pe.wait_ge(s_acc, SLOTT)
            rounds(pe, TURNS // 2, router_turns)

            pe.wait_ge(s_wback, 16 * EXPERTS)
            pe.wait_ge(s_etab, 1)

            def pairs_mm(dst_ap, left, right, first, last_one):
                for n, (a, b) in enumerate(((0, 0), (0, 1), (1, 0))):
                    ins = mm(dst_ap, left[a], right[b], start=first and n == 0, stop=last_one and n == 2,
                             skip_group_check=True)
                return ins

            def turn_rows(i):
                for sub in range(2):
                    bT = bank[4 * sub][:, :].bitcast(F16).rearrange("p (q h n) -> p q h n", q=4, h=2)
                    pe.wait_ge(s_exin[sub], 16 * (i + 1))
                    for h in range(2):
                        for q in range(4):
                            last = nc.tensor.transpose(bT[:, q, h, :], ex_x[:, sub, h, q * P:(q + 1) * P],
                                                       ident16[:, :])
                    last.then_inc(s_exT_pe[sub], 1)

            turn_rows(0)

            def expert_step(i):
                exp = loads(pe, tile_expert[0:1, bass.ds(2 * i, 2)], EXPERTS - 1)
                for sub in range(2):
                    xT = ex_xT[:, sub, :].rearrange("p (w k n) -> p w k n", w=2, k=KD)
                    pe.wait_ge(s_exT_act[sub], i + 1)
                    for c in range(KH):
                        for k in range(KD):
                            w = [t[:, bass.ds(exp[sub], 1), k, c * P:(c + 1) * P].rearrange("p a n -> p (a n)")
                                 for t in (w1h, w1l)]
                            last = pairs_mm(bank[4 * sub + 1 + c // 2][:, c % 2 * EROWS:(c % 2 + 1) * EROWS],
                                            w, [xT[:, 0, k, :], xT[:, 1, k, :]], k == 0, k == KD - 1)
                        if c % 2:
                            last.then_inc(s_ex_pe[sub], 1)
                if not is_last(i, NE // 2):
                    turn_rows(i + 1)
                for sub in range(2):
                    pe.wait_ge(s_ex_dve[sub], done(EX_DVE, "low_b", i))
                    for h in range(2):
                        for c in range(KH):
                            at = c * EROWS + h * P
                            w = [t[:, bass.ds(exp[sub], 1), c, :].rearrange("p a n -> p (a n)")
                                 for t in (w2h, w2l)]
                            last = pairs_mm(bank[4 * sub + 3][:, h * D:(h + 1) * D],
                                            [ex_hh[:, sub, at:at + P], ex_hl[:, sub, at:at + P]], w,
                                            c == 0, c == KH - 1)
                    last.then_inc(s_ex_pe[sub], 1)

            rounds(pe, NE // 2, expert_step)

        @block.scalar
        def _(act):
            a = nc.scalar
            act.wait_ge(s_made, 7)

            def std_of(sub, s, wait_sem, value):
                act.wait_ge(wait_sem, value)
                a.activation(std[:, sub, :], mv[:, sub, 1:2], ACT.Sqrt, bias=eps[:, 0:1]).then_inc(s, 1)

            act.wait_ge(s_b1T, 1)
            a.copy(b1T[:, :], bank[7][:, 0:EXPERTS * KH]).then_inc(s_b1c, 1)

            def ln_tile(i):
                def take_T(sub):
                    act.wait_ge(s_ln_pe[sub], done(LN_PE, "nT", i))
                    a.copy(normedT[:, sub, :], bank[2 + sub][:, 0:D]).then_inc(s_ln_act[sub], 1)

                def take_h(sub):
                    if not is_first(i):
                        act.wait_ge(s_hst[sub], 16 * i)
                    act.wait_ge(s_ln_pe[sub], done(LN_PE, "h", i))
                    a.copy(h_out[:, sub, :], bank[4 + sub][:, 0:D]).then_inc(s_ln_act[sub], 1)

                std_of(0, s_ln_act[0], s_ln_dve[0], done(LN_DVE, "aggr", i))
                take_T(0)
                std_of(1, s_ln_act[1], s_ln_dve[1], done(LN_DVE, "aggr", i))
                take_h(0)
                take_T(1)
                take_h(1)

            def store_pairs(i):
                held(act, "act", s_wlow, 4 * (i - 1))
                for b in range(2):
                    act.dma_start(weight_pairs[bass.ds(2 * (i - 2) + b, 1)].rearrange("a p m -> p (a m)"),
                                  made[:, b].rearrange("p w m -> p (w m)")).then_inc(s_wst, 16)

            def load_weights(i):
                for b in range(2):
                    e = bass.ds(2 * (i - 1) + b, 1)
                    act.dma_start(w_in[:, b, 0, :].rearrange("p (k n) -> p k n", k=KD),
                                  w1[e].rearrange("a (k p) n -> p (a k) n", p=P)).then_inc(s_win[b], 16)
                    act.dma_start(w_in[:, b, 1, :].rearrange("p (k n) -> p k n", k=KH),
                                  w2[e].rearrange("a (k p) n -> p (a k) n", p=P)).then_inc(s_win[b], 16)

            def high_weights(i):
                for b in range(2):
                    held(act, "act", s_win[b], 32 * i)
                    if not (isinstance(i, int) and i == 1):
                        held(act, "act", s_wst, 32 * (i - 1))
                    for w in range(2):
                        a.activation(made[:, b, 2 * w, :], w_in[:, b, w, :], ACT.Copy,
                                     scale=WSCALE).then_inc(s_whigh, 1)

            ln_tile(0)
            act.wait_ge(s_based, 2)
            load_weights(1)
            ln_tile(1)
            high_weights(1)
            with act.Fori(2, SPLITS + 1) as i:
                store_pairs(i)
                load_weights(i)
                ln_tile(i)
                high_weights(i)
            store_pairs(SPLITS + 1)
            with act.Fori(SPLITS + 1, NP_ - 1) as i:
                ln_tile(i)
            ln_tile(NP_ - 1)

            def std_x1_of(n):
                act.wait_ge(s_stats, 2 * n + 2)
                a.activation(std_2[:, :], mv_2[:, :, 1], ACT.Sqrt, bias=eps[:, 0:1]).then_inc(s_stdx, 1)

            std_x1_of(0)
            act.wait_ge(s_scale, 2)

            def y_of(turn, b):
                for k in range(LANES):
                    at = LANES * turn + k
                    a.activation(y_rt[:, b, k, :], acc[:, bass.ds(at, 1), :].rearrange("p a d -> p (a d)"),
                                 ACT.Identity, bias=shift_x1[:, bass.ds(at, 1)],
                                 scale=rstd_x1[:, bass.ds(at, 1)]).then_inc(s_y, 1)

            def ratio_of(turn):
                act.wait_ge(s_less, turn + 1)
                a.activation(ratio[:, :], less[:, :], ACT.Exp).then_inc(s_ratio, 1)

            y_of(0, 0)

            def router_turns(i):
                for b in range(2):
                    turn = 2 * i + b
                    more = not is_last(i, TURNS // 2)
                    if more and b:
                        std_x1_of(i + 1)
                    act.wait_ge(s_rt_dve, done(RT_DVE, "aggr", turn))
                    a.activation(std_rt[:, :], mv_rt[:, :, 1], ACT.Sqrt, bias=eps[:, 0:1]).then_inc(s_rt_act, 1)
                    act.wait_ge(s_rt_dve, done(RT_DVE, "shift", turn))
                    for k in range(LANES):
                        last = a.activation(y_rt[:, b, k, :], y_rt[:, b, k, :], ACT.Identity,
                                            bias=shift_rt[:, k:k + 1], scale=rstd_rt[:, k:k + 1])
                    last.then_inc(s_z, 1)
                    if more or b == 0:
                        if b:
                            held(act, "act", s_scale, 2 * i + 4)
                        if not (is_first(i) and b == 0):
                            held(act, "act", s_low, turn)
                        y_of(turn + 1, 1 - b)
                    if not (is_first(i) and b == 0):
                        ratio_of(turn - 1)
                    if not is_first(i):
                        held(act, "act", s_disp[b], 32 * LANES * i)
                    act.wait_ge(s_rt_dve, done(RT_DVE, "xn", turn))
                    a.copy(pairs[:, b, :, 0:D], y_rt[:, b]).then_inc(s_rt_act, 1)
                    for k in range(0, LANES, 2):
                        n = min(2, LANES - k)
                        act.wait_ge(s_rtT_pe, lane_banks * turn + k // 2 + 1)
                        a.copy(xnT_rt[:, k:k + n, :],
                               bank[k // 2][:, 0:n * D].rearrange("p (s n) -> p s n", s=n)).then_inc(s_rtT_act, 1)

            rounds(act, TURNS // 2, router_turns)
            ratio_of(TURNS - 1)

            act.wait_ge(s_etab, 1)
            act.wait_ge(s_wlow, 2 * EXPERTS)
            act.wait_ge(s_b1c, 1)

            def take_xT(i):
                for sub in range(2):
                    act.wait_ge(s_exT_pe[sub], i + 1)
                    a.copy(ex_xT[:, sub, :], bank[4 * sub][:, :].bitcast(F16)).then_inc(s_exT_act[sub], 1)

            take_xT(0)

            def expert_step(i):
                exp = loads(act, tile_expert[0:1, bass.ds(2 * i, 2)], EXPERTS - 1)
                for sub in range(2):
                    for half in range(2):
                        held(act, "act", s_ex_pe[sub], done(EX_PE, ("up_a", "up_b")[half], i))
                        for c in range(2 * half, 2 * half + 2):
                            last = a.activation(ex_h[:, sub, c * EROWS:(c + 1) * EROWS],
                                                bank[4 * sub + 1 + half][:, c % 2 * EROWS:(c % 2 + 1) * EROWS],
                                                ACT.Gelu, bias=b1T[:, bass.ds(exp[sub] * KH + c, 1)],
                                                scale=1.0 / WSCALE)
                        last.then_inc(s_ex_act[sub], 1)
                if not is_last(i, NE // 2):
                    take_xT(i + 1)

            rounds(act, NE // 2, expert_step)

        @block.vector
        def _(dve):
            v = nc.vector
            link_count = [0]

            def link(ins, s=s_mid):
                link_count[0] += 1
                ins.then_inc(s, 1)
                dve.wait_ge(s, link_count[0])

            v.memset(src_sb[:, :], NT * P).then_inc(s_made, 1)
            v.memset(dst_sb[:, :], 0).then_inc(s_made, 1)
            v.memset(ew_sb[:, :], 0.0).then_inc(s_made, 1)
            v.memset(ones[:, :], 1.0).then_inc(s_made, 1)
            v.memset(onesf[:, :], 1.0).then_inc(s_made, 1)
            v.memset(eps[:, :], EPS).then_inc(s_made, 1)
            v.memset(xin[:, :, :], 0.0).then_inc(s_made, 1)
            v.memset(chosen[:, :, :], 0.0)
            link(v.memset(fill[:, :, :], 0))
            v.memset(fill_f[:, :, 1], 2.0 * P)
            v.memset(fill[:, :, 0], FAR).then_inc(s_zero, 1)
            link(v.memset(empty[:, :, :], 0))
            dve.wait_ge(s_numbers, 3)
            v.tensor_copy(empty[:, :, :].bitcast(F32)[:, :, D], spare[:, :]).then_inc(s_zero, 1)
            dve.wait_ge(s_const, 1)
            link(v.tensor_copy(ramp[:, :], ramp_i))
            dve.wait_ge(s_src, 32)
            link(v.tensor_scalar(ramp_i[:, 0:COLS], src_sb[:, :], 7, None, ALU.arith_shift_right))
            v.tensor_copy(bins16[:, :], ramp_i[:, 0:COLS]).then_inc(s_recs, 1)
            link(v.tensor_scalar(src_sb[:, :], src_sb[:, :], P - 1, None, ALU.bitwise_and))
            v.tensor_copy(recs_f[:, :, 1], src_sb[:, :]).then_inc(s_recs, 1)
            dve.wait_ge(s_edge, 64)
            v.tensor_copy(recs[:, :, 0], dst_sb[:, :]).then_inc(s_recs, 1)
            v.tensor_copy(recs_f[:, :, 2], ew_sb[:, :]).then_inc(s_recs, 1)
            v.memset(recs[:, :, 3], 0).then_inc(s_recs, 1)
            dve.wait_ge(s_recs, 5)
            link(v.tensor_scalar(em8[:, :], ramp[:, 0:EXPERTS], float(EXPERTS), None, ALU.subtract))
            dve.wait_ge(s_const, 9)
            link(v.tensor_copy(ident16[:, :], ident[:, :]))
            v.sem_inc(s_cleared, 1)
            dve.wait_ge(s_par, 16 * 6)

            def one_hot(t, tile_hot):
                cols = bins16[:, bass.ds(PER * t, PER)].unsqueeze(1).broadcast_to([P, BINS, PER])
                v.tensor_tensor(tile_hot, numbers[:, :, :], cols, ALU.is_equal).then_inc(s_hot, 1)

            def hist_step(i):
                for k, tile_hot in enumerate(hist_hot):
                    if not is_first(i):
                        dve.wait_ge(s_hist, LANES * i - LANES + k + 1)
                    one_hot(LANES * i + k, tile_hot)

            rounds(dve, TURNS, hist_step)

            dve.wait_ge(s_hist, NT)
            for b in range(2):
                link(v.tensor_copy(totals[:, GRP * b:GRP * b + GRP, :], counts(b).rearrange("p b c -> p c b")))
            link(v.tensor_reduce(binsum[:, :], totals[:, :, :].rearrange("p c b -> p b c"), AX_X, ALU.add))
            link(v.tensor_scalar(binsum[:, :], binsum[:, :], float(P - 1), None, ALU.add))
            link(v.tensor_copy(bintile_i[:, :], binsum[:, :]))
            link(v.tensor_scalar(bintile_i[:, :], bintile_i[:, :], 7, None, ALU.arith_shift_right))
            link(v.tensor_copy(bintile[:, :], bintile_i[:, :]))
            link(v.tensor_tensor_scan(binend[:, :], onesf[:, 0:BINS], bintile[:, :], 0.0, ALU.mult, ALU.add))
            v.sem_inc(s_ends, 1)
            link(v.tensor_tensor(binsum[:, :], binend[:, :], bintile[:, :], ALU.subtract))
            link(v.tensor_scalar(base[:, 0, :], binsum[:, :], float(P), None, ALU.mult))
            for c in range(1, CHAINS):
                link(v.tensor_tensor(base[:, c, :], base[:, c - 1, :], totals[:, c - 1, :], ALU.add))
            link(v.memset(base[:, :, NT:BINS], BEYOND))
            v.sem_inc(s_base, 1)
            dve.wait_ge(s_colT, 1)
            link(v.tensor_copy(endcol[0:NT, :], bank[2][0:NT, 0:1]))
            v.tensor_scalar(past[0:NT, :], ramp[0:NT, :], endcol[0:NT, 0:1], None, ALU.is_ge).then_inc(s_past, 1)
            quarter = SLOTT // 4
            for q in range(4):
                dve.wait_ge(s_tbl, 4)
                v.tensor_scalar(tile_bin[0:1, q * quarter:(q + 1) * quarter], bank[3 + q][0:1, 0:quarter],
                                float(NT - 1), None, ALU.min).then_inc(s_tbl, 1)

            def positions(i, sub):
                t = 2 * i + sub
                dve.wait_ge(s_red, GRPS * t + GRPS)
                v.tensor_copy(pos_i[:, sub, :], pos[:, sub, :]).then_inc(s_pos, 1)
                dve.wait_ge(s_pos, done(POS, "int", t))
                v.tensor_scalar(pos_row[:, sub, :], pos_i[:, sub, :], P - 1, None, ALU.bitwise_and).then_inc(s_pos, 1)
                v.tensor_scalar(pos_col[:, sub, :], pos_i[:, sub, :], 7, None, ALU.arith_shift_right).then_inc(s_pos, 1)
                dve.wait_ge(s_pos, done(POS, "col", t))
                if not is_first(i):
                    dve.wait_ge(s_scat[sub], 16 * PER * i)
                v.scalar_tensor_tensor(out=addr[:, sub, :], in0=pos_row[:, sub, :], scalar=float(SLOTT),
                                       in1=pos_col[:, sub, :], op0=ALU.mult, op1=ALU.add).then_inc(s_pos, 1)
                v.tensor_copy(rec_out[:, sub, :, :], recs[:, bass.ds(PER * t, PER), :]).then_inc(s_pos, 1)

            def held_aggr(s, sub, value):
                held(dve, "dve", s, value)
                v.bn_aggr(mv[:, sub, :], stats[:, sub, :]).then_inc(s, 1)

            def sort_step(i):
                for sub in range(2):
                    t = 2 * i + sub
                    s = s_ln_dve[sub]

                    def extract(gidx):
                        dve.wait_ge(s_rank, GRPS * t + gidx + 1)
                        v.tensor_tensor(prod[:, gidx % 2, :, :], hot_of(sub, gidx), counts(gidx % 2),
                                        ALU.mult).then_inc(s_read, 1)
                        dve.wait_ge(s_read, GRPS * t + gidx + 1)
                        v.tensor_reduce(pos[:, sub, GRP * gidx:GRP * gidx + GRP],
                                        prod[:, gidx % 2, :, :].rearrange("p b c -> p c b"),
                                        AX_X, ALU.add).then_inc(s_red, 1)

                    if not is_first(i):
                        dve.wait_ge(s_count, GRPS * (t - 1))
                    one_hot(t, hot[:, sub])
                    dve.wait_ge(s_xin[sub], 16 * (i + 1))
                    v.bn_stats(stats[:, sub, :], xin[:, sub, :]).then_inc(s, 1)
                    v.tensor_tensor(acc[:, bass.ds(t, 1), :].rearrange("p a d -> p (a d)"), xin[:, sub, :],
                                    gb_sb[:, :], ALU.add)
                    extract(0)
                    held_aggr(s, sub, done(LN_DVE, "stats", i))
                    extract(1)
                    extract(2)
                    dve.wait_ge(s_ln_act[sub], done(LN_ACT, "std", i))
                    v.reciprocal(rstd[:, sub, :], std[:, sub, :]).then_inc(s, 1)
                    extract(3)
                    dve.wait_ge(s, done(LN_DVE, "rstd", i))
                    if not is_first(i):
                        dve.wait_ge(s_ln_pe[sub], done(LN_PE, "nT", i - 1))
                    v.tensor_scalar(normed[:, sub, :], xin[:, sub, :], mv[:, sub, 0:1], rstd[:, sub, 0:1],
                                    ALU.subtract, ALU.mult).then_inc(s, 1)
                    positions(i, sub)

            def low_weights(i):
                for b in range(2):
                    for w in range(2):
                        held(dve, "dve", s_whigh, 4 * (i - 1) + 2 * b + w + 1)
                        v.scalar_tensor_tensor(out=made[:, b, 2 * w + 1, :], in0=w_in[:, b, w, :], scalar=WSCALE,
                                               in1=made[:, b, 2 * w, :], op0=ALU.mult,
                                               op1=ALU.subtract).then_inc(s_wlow, 1)

            sort_step(0)
            with dve.Fori(1, SPLITS + 1) as i:
                sort_step(i)
                low_weights(i)
            dve.wait_ge(s_wlow, 2 * EXPERTS)
            v.memset(rows[:, :, :], 0.0).then_inc(s_cleared, 1)
            dve.wait_ge(s_wst, 16 * EXPERTS)
            with dve.Fori(SPLITS + 1, NP_ - 1) as i:
                sort_step(i)
            sort_step(NP_ - 1)

            def make_pick(i, sub, k):
                n = PER * (2 * i + sub) + k
                if k == 0:
                    dve.wait_ge(s_recin[sub], 16 * (i + 1))
                if not (is_first(i) and sub == 0 and k < 4):
                    dve.wait_ge(s_sum, n - 3)
                v.tensor_scalar(pick[:, k % 4, :], ramp[:, 0:P], rec_in_f[:, sub, k, 1:2],
                                rec_in_f[:, sub, k, 2:3], ALU.is_equal, ALU.mult).then_inc(s_pick, 1)

            def add_sum(i, sub, k, where):
                n = PER * (2 * i + sub) + k
                place = acc[:, bass.ds(where, 1), :].rearrange("p a d -> p (a d)")
                dve.wait_ge(s_sum, n + 1)
                if not (is_first(i) and sub == 0 and k == 0):
                    dve.wait_ge(s_acc, n)
                v.tensor_tensor(place, place, bank[k % 4][:, 0:D], ALU.add).then_inc(s_acc, 1)

            def sum_step(i):
                for sub in range(2):
                    make_pick(i, sub, 0)
                    make_pick(i, sub, 1)
                    where = loads(dve, tile_bin[0:1, bass.ds(PER * (2 * i + sub), PER)], NT - 1)
                    for k in range(PER):
                        if k + 2 < PER:
                            make_pick(i, sub, k + 2)
                        add_sum(i, sub, k, where[k])

            dve.wait_ge(s_tbl, 8)
            dve.wait_ge(s_cleared, 2)
            rounds(dve, STEPS // 2, sum_step)

            dve.wait_ge(s_acc, SLOTT)

            def stats_x1(n):
                for k in range(2 * LANES):
                    last = v.bn_stats(stats_2[:, k, :], acc[:, bass.ds(2 * LANES * n + k, 1), :]
                                      .rearrange("p a d -> p (a d)"))
                last.then_inc(s_stats, 1)
                held(dve, "dve", s_stats, 2 * n + 1)
                for k in range(2 * LANES):
                    last = v.bn_aggr(mv_2[:, k, :], stats_2[:, k, :])
                last.then_inc(s_stats, 1)

            def scale_x1(n):
                dve.wait_ge(s_stdx, n + 1)
                v.reciprocal(rstd_2[:, :], std_2[:, :]).then_inc(s_rstdx, 1)
                dve.wait_ge(s_rstdx, n + 1)
                turns = bass.ds(2 * LANES * n, 2 * LANES)
                v.tensor_copy(rstd_x1[:, turns], rstd_2[:, :]).then_inc(s_scale, 1)
                v.scalar_tensor_tensor(out=shift_x1[:, turns], in0=mv_2[:, :, 0], scalar=-1.0, in1=rstd_2[:, :],
                                       op0=ALU.mult, op1=ALU.mult).then_inc(s_scale, 1)

            stats_x1(0)
            link(v.tensor_scalar(taken[:, :], em8[:, :], float(EXPERTS), float(ECAP), ALU.add, ALU.mult))
            scale_x1(0)

            def over_experts(ap):
                return ap.unsqueeze(2).broadcast_to([P, LANES, EXPERTS])

            wide_gamma, wide_beta = (t[:, :].unsqueeze(1).broadcast_to([P, LANES, D]) for t in (gamma_sb, beta_sb))

            def over_lanes(ap):
                return ap.unsqueeze(1).broadcast_to([P, LANES, EXPERTS])

            def low_parts(turn, b):
                dve.wait_ge(s_rt_act, done(RT_ACT, "high", turn))
                v.tensor_tensor(pairs[:, b, :, D:HL], y_rt[:, b], pairs[:, b, :, 0:D], ALU.subtract).then_inc(s_low, 1)

            def top_two(turn, last_turn):
                def top(name, ins):
                    ins.then_inc(s_top, 1)
                    dve.wait_ge(s_top, done(TOP, name, turn))

                def largest(c, values):
                    n = c + 1
                    top(f"max{n}", v.tensor_reduce(vals[:, c, :], values, AX_X, ALU.max))
                    top(f"equal{n}", v.tensor_tensor(hots[:, c], values, over_experts(vals[:, c, :]), ALU.is_equal))
                    top(f"number{n}", v.tensor_tensor(hots[:, c], hots[:, c], over_lanes(em8[:, :]), ALU.mult))
                    top(f"first{n}", v.tensor_reduce(first[:, c, :], hots[:, c], AX_X, ALU.min))
                    top(f"hot{n}", v.tensor_tensor(hots[:, c], over_lanes(em8[:, :]), over_experts(first[:, c, :]),
                                                   ALU.is_equal))

                dve.wait_ge(s_lg_pe, turn + 1)
                top("logits", v.tensor_tensor(
                    logits[:, :, :], bank[4][:, 0:LANES * EXPERTS].rearrange("p (t e) -> p t e", e=EXPERTS),
                    over_lanes(br_sb[:, :]), ALU.add))
                largest(0, logits[:, :, :])
                top("masked", v.scalar_tensor_tensor(out=masked[:, :, :], in0=hots[:, 0], scalar=-HUGE,
                                                     in1=logits[:, :, :], op0=ALU.mult, op1=ALU.add))
                largest(1, masked[:, :, :])
                if last_turn:
                    v.tensor_scalar(hots[:, :, LANES - 1, :], hots[:, :, LANES - 1, :], valid[:, 0:1], None,
                                    ALU.mult).then_inc(s_valid, 1)
                    dve.wait_ge(s_valid, 1)
                v.tensor_tensor(chosen[:, 0:LANES, :], hots[:, 0], hots[:, 1], ALU.add).then_inc(s_top, 1)
                v.tensor_tensor(less[:, :], vals[:, 1, :], vals[:, 0, :], ALU.subtract).then_inc(s_less, 1)

            def places(turn, b, earlier):
                def place(name, ins):
                    ins.then_inc(s_place, 1)
                    dve.wait_ge(s_place, done(PLACE, name, turn))

                dve.wait_ge(s_prefix, turn + 1)
                counted = bank[5][:, 0:(LANES + 1) * EXPERTS].rearrange("p (t e) -> p t e", e=EXPERTS)
                place("slot", v.tensor_tensor(slot[:, :, :], counted[:, 0:LANES, :], over_lanes(taken[:, :]), ALU.add))
                v.tensor_tensor(taken[:, :], taken[:, :], counted[:, LANES, :], ALU.add).then_inc(s_place, 1)
                place("own", v.tensor_tensor(own[:, :, :, :], hots[:, :, :, :],
                                             slot[:, :, :].unsqueeze(1).broadcast_to([P, 2, LANES, EXPERTS]), ALU.mult))
                place("sum", v.tensor_reduce(own_slot[:, :, :], own[:, :, :, :], AX_X, ALU.add))
                if earlier is not None:
                    held(dve, "dve", s_disp[b], 32 * LANES * earlier)
                v.tensor_copy(slot_st[:, b], own_slot[:, :, :]).then_inc(s_place, 1)
                v.tensor_copy(notes[:, b, :, 0], node[:, :]).then_inc(s_gates, 1)
                v.tensor_scalar(node[:, :], node[:, :], float(LANES * P), None, ALU.add).then_inc(s_gates, 1)
                v.tensor_copy(notes[:, b, :, 1], first[:, 0, :]).then_inc(s_gates, 1)
                dve.wait_ge(s_ratio, turn + 1)
                v.tensor_scalar(total[:, :], ratio[:, :], 1.0, None, ALU.add).then_inc(s_gates, 1)
                dve.wait_ge(s_gates, done(GATES, "total", turn))
                v.reciprocal(notes[:, b, :, 2], total[:, :]).then_inc(s_gates, 1)
                dve.wait_ge(s_gates, done(GATES, "gate1", turn))
                v.tensor_tensor(notes[:, b, :, 3], notes[:, b, :, 2], ratio[:, :], ALU.mult).then_inc(s_gates, 1)

            def router_turns(i):
                for b in range(2):
                    turn = 2 * i + b
                    first_turn = is_first(i) and b == 0

                    def lanes(one):
                        for k in range(LANES):
                            last = one(k)
                        last.then_inc(s_rt_dve, 1)

                    def stats_of(k):
                        dve.wait_ge(s_y, LANES * turn + k + 1)
                        return v.bn_stats(stats_rt[:, k, :], y_rt[:, b, k, :])

                    lanes(stats_of)
                    held(dve, "dve", s_rt_dve, done(RT_DVE, "stats", turn))
                    lanes(lambda k: v.bn_aggr(mv_rt[:, k, :], stats_rt[:, k, :]))
                    if not first_turn:
                        low_parts(turn - 1, 1 - b)
                    dve.wait_ge(s_rt_act, done(RT_ACT, "std", turn))
                    v.reciprocal(rstd_rt[:, :], std_rt[:, :]).then_inc(s_rt_dve, 1)
                    dve.wait_ge(s_rt_dve, done(RT_DVE, "rstd", turn))
                    v.scalar_tensor_tensor(out=shift_rt[:, :], in0=mv_rt[:, :, 0], scalar=-1.0, in1=rstd_rt[:, :],
                                           op0=ALU.mult, op1=ALU.mult).then_inc(s_rt_dve, 1)
                    if not first_turn:
                        if b and not is_last(i, TURNS // 2):
                            scale_x1(i + 1)
                        top_two(turn - 1, False)
                    dve.wait_ge(s_z, turn + 1)
                    v.tensor_tensor(y_rt[:, b], y_rt[:, b], wide_gamma, ALU.mult).then_inc(s_rt_dve, 1)
                    dve.wait_ge(s_rt_dve, done(RT_DVE, "scaled", turn))
                    v.tensor_tensor(y_rt[:, b], y_rt[:, b], wide_beta, ALU.add).then_inc(s_rt_dve, 1)
                    if not first_turn:
                        if is_first(i):
                            earlier = None
                        elif b == 0:
                            earlier = None if isinstance(i, int) and i == 1 else i - 1
                        else:
                            earlier = i
                        places(turn - 1, 1 - b, earlier)
                    if not is_last(i, TURNS // 2):
                        if b == 0:
                            stats_x1(i + 1)

            router_turns(0)
            router_turns(1)
            with dve.Fori(2, TURNS // 2 - 1) as i:
                router_turns(i)
            router_turns(TURNS // 2 - 1)
            low_parts(TURNS - 1, 1)
            top_two(TURNS - 1, True)
            places(TURNS - 1, 1, TURNS // 2 - 1)
            dve.wait_ge(s_place, done(PLACE, "int", TURNS - 1))

            v.tensor_copy(taken_i[:, :], taken[0:1, :]).then_inc(s_tail, 1)
            link(v.tensor_scalar(gap[:, :], em8[:, :], float(EXPERTS), float(ECAP), ALU.add, ALU.mult))
            link(v.tensor_tensor(count[:, :], taken[:, :], gap[:, :], ALU.subtract))
            link(v.tensor_scalar(count[:, :], count[:, :], float(EROWS - 1), None, ALU.add))
            link(v.tensor_copy(etile_i[:, :], count[:, :]))
            link(v.tensor_scalar(etile_i[:, :], etile_i[:, :], 8, None, ALU.arith_shift_right))
            link(v.tensor_copy(etile[:, :], etile_i[:, :]))
            link(v.tensor_tensor_scan(eend[:, :], onesf[:, 0:EXPERTS], etile[:, :], 0.0, ALU.mult, ALU.add))
            steps = ramp[0:1, 0:NE]
            link(v.tensor_tensor(ended, steps.unsqueeze(2).broadcast_to([1, NE, EXPERTS]),
                                 eend[0:1, :].unsqueeze(1).broadcast_to([1, NE, EXPERTS]), ALU.is_ge))
            link(v.tensor_reduce(tile_sum[:, :], ended, AX_X, ALU.add))
            link(v.tensor_scalar(tile_expert[:, :], tile_sum[:, :], float(EXPERTS - 1), None, ALU.min))
            link(v.tensor_scalar(gap[:, :], etile[:, :], -1.0, float(ECAP // EROWS), ALU.mult, ALU.add))
            link(v.tensor_tensor(ended, ended, gap[0:1, :].unsqueeze(1).broadcast_to([1, NE, EXPERTS]), ALU.mult))
            link(v.tensor_reduce(tile_sum[:, :], ended, AX_X, ALU.add))
            link(v.tensor_tensor(tile_sum[:, :], tile_sum[:, :], steps, ALU.add))
            link(v.tensor_scalar(tile_block[:, :], tile_sum[:, :], float(ZERO_AT // EROWS), None, ALU.min))
            v.sem_inc(s_etab, 1)

            dve.wait_ge(s_b2, 16)
            dve.wait_ge(s_etab, 1)

            def take_notes(i):
                for sub in range(2):
                    dve.wait_ge(s_exin[sub], 16 * (i + 1))
                    v.tensor_copy(note[:, sub], ex_row[:, sub, :, D:ROW]).then_inc(s_note[sub], 1)

            take_notes(0)

            def expert_step(i):
                exp = loads(dve, tile_expert[0:1, bass.ds(2 * i, 2)], EXPERTS - 1)
                for sub in range(2):
                    dve.wait_ge(s_note[sub], i + 1)
                    v.tensor_scalar(is_top[:, sub, :], note[:, sub, :, 1], em8[:, bass.ds(exp[sub], 1)], None,
                                    ALU.is_equal).then_inc(s_pass, 1)
                dve.wait_ge(s_pass, 4 * i + 2)
                v.tensor_tensor(gate_top[:, :, :], is_top[:, :, :], note[:, :, :, 2], ALU.mult).then_inc(s_pass, 1)
                v.scalar_tensor_tensor(out=gate_second[:, :, :], in0=is_top[:, :, :], scalar=1.0, in1=note[:, :, :, 3],
                                       op0=ALU.subtract, op1=ALU.mult).then_inc(s_pass, 1)
                dve.wait_ge(s_pass, 4 * i + 4)
                v.tensor_tensor(gate[:, :, :], gate_top[:, :, :], gate_second[:, :, :], ALU.subtract)
                v.tensor_copy(ex_node[:, :, :], note[:, :, :, 0])
                for sub in range(2):
                    for half in range(2):
                        part = slice(half * 2 * EROWS, (half + 1) * 2 * EROWS)
                        dve.wait_ge(s_ex_act[sub], done(EX_ACT, ("gelu_a", "gelu_b")[half], i))
                        v.tensor_copy(ex_hh[:, sub, part], ex_h[:, sub, part]).then_inc(s_ex_dve[sub], 1)
                        dve.wait_ge(s_ex_dve[sub], done(EX_DVE, ("high_a", "high_b")[half], i))
                        v.tensor_tensor(ex_hl[:, sub, part], ex_h[:, sub, part], ex_hh[:, sub, part],
                                        ALU.subtract).then_inc(s_ex_dve[sub], 1)
                if not is_last(i, NE // 2):
                    take_notes(i + 1)
                for sub in range(2):
                    if not is_first(i):
                        held(dve, "dve", s_exst[sub], 32 * i)
                    dve.wait_ge(s_ex_pe[sub], done(EX_PE, "down", i))
                    v.scalar_tensor_tensor(
                        out=ex_y[:, sub], in0=bank[4 * sub + 3][:, :].rearrange("p (h n) -> p h n", h=2),
                        scalar=1.0 / WSCALE, in1=b2_sb[:, bass.ds(exp[sub], 1), :].broadcast_to([P, 2, D]),
                        op0=ALU.mult, op1=ALU.add).then_inc(s_ex_dve[sub], 1)
                    v.tensor_copy(node_st[:, sub, :], ex_node[:, sub, :])
                    dve.wait_ge(s_ex_dve[sub], done(EX_DVE, "y", i))
                    for h in range(2):
                        last = v.tensor_scalar(ex_y[:, sub, h, :], ex_y[:, sub, h, :], gate[:, sub, h:h + 1], None,
                                               ALU.mult)
                    last.then_inc(s_ex_dve[sub], 1)

            rounds(dve, NE // 2, expert_step)


_INS = ['x', 'src', 'dst', 'edge_weight', 'L0_gnn_weight', 'L0_gnn_b', 'L0_ffn_gamma', 'L0_ffn_beta',
        'L0_ffn_Wr', 'L0_ffn_br', 'L0_ffn_W1', 'L0_ffn_b1', 'L0_ffn_W2', 'L0_ffn_b2']


def kernel(**inputs):
    import numpy as _np
    import concourse.bacc as _bacc
    from concourse import mybir as _mybir
    from concourse.bass_utils import run_bass_kernel_spmd as _run

    nc = _bacc.Bacc("TRN2", target_bir_lowering=False, num_devices=1)
    arrays, args = {}, []
    for name in _INS:
        a = _np.ascontiguousarray(inputs[name])
        arrays[f"in_{name}_dram"] = a
        args.append(nc.dram_tensor(f"in_{name}_dram", a.shape, _mybir.dt.from_np(a.dtype), kind="ExternalInput").ap())
    args.append(nc.dram_tensor("out_0_dram", (NODES, D), _mybir.dt.float32, kind="ExternalOutput").ap())
    gnn_moe(nc, *args)
    r = _run(nc, [arrays], core_ids=[0])
    return r.results[0]["out_0_dram"]
```
